# Optimizing a Trainium2 kernel written in Bass

```python
import numpy as np
import jax
import jax.numpy as jnp

def _softmax(x, axis=-1):
    return jax.nn.softmax(x, axis=axis)

def _gelu(x):
    return jax.nn.gelu(x, approximate=True)

def _silu(x):
    return jax.nn.silu(x)

def _sigmoid(x):
    return jax.nn.sigmoid(x)

def _layernorm(x, axis=-1, eps=1e-05):
    m = jnp.mean(x, axis=axis, keepdims=True)
    v = jnp.var(x, axis=axis, keepdims=True)
    return (x - m) / jnp.sqrt(v + eps)

def _scatter_add(tgt, idx, src, axis=0):
    return tgt.at[idx].add(src)

def _segment_sum(src, seg, n):
    return jax.ops.segment_sum(src, seg, n)
kernel_name = 'mk_cond_resid_d1_seqx_r8_c0465b'

def setup_inputs(seed: int=0):
    np.random.seed(seed)
    _w = jnp.asarray

    def _rec_inputs():
        import jax
        import jax.numpy as jnp
        _rk = jax.random.key(seed)
        x = 7.22e-05 + 1 * jax.random.normal(jax.random.fold_in(_rk, 1), (32, 128, 128), jnp.float32)
        _lenS = 128 - jax.random.randint(jax.random.fold_in(_rk, 7), (32,), 0, max(1, 128 // 4) + 1, jnp.int32)
        _lenS2 = 128 - jax.random.randint(jax.random.fold_in(_rk, 8), (32,), 0, max(1, 128 // 4) + 1, jnp.int32)
        cond_256 = 0.000887014 + 1.03683 * jax.random.normal(jax.random.fold_in(_rk, 11), (32, 32), jnp.float32)
        return (x, cond_256)
    x, cond_256 = _rec_inputs()

    def _L0_cond_setup():
        import jax, jax.numpy as jnp
        import numpy as np
        D_MODEL = 128
        D_T = 32
        N_HEADS = 16
        HIDDEN = 4 * D_MODEL
        EPS = 1e-06

        def _tc_rmsnorm(x, t, gw, gb, bw, bb):
            g = (t @ gw.T + gb)[:, None, :]
            b = (t @ bw.T + bb)[:, None, :]
            inv_rms = jax.lax.rsqrt(jnp.mean(x * x, axis=-1, keepdims=True) + EPS)
            return g * x * inv_rms + b

        def _attention(x, Wq, Wk, Wv, Wo):
            B, L, D = x.shape
            H = N_HEADS
            dh = D // H
            scale = np.sqrt(dh).astype(np.float32)
            q = (x @ Wq.T).reshape(B, L, H, dh)
            k = (x @ Wk.T).reshape(B, L, H, dh)
            v = (x @ Wv.T).reshape(B, L, H, dh)
            attn = jnp.einsum('blhd,bmhd->bhlm', q, k) / scale
            p = jax.nn.softmax(attn, axis=-1)
            o = jnp.einsum('bhlm,bmhd->blhd', p, v).reshape(B, L, D)
            return o @ Wo.T

        def _swiglu(x, gate_w, hid_w, out_w):
            return jax.nn.silu(x @ gate_w.T) * (x @ hid_w.T) @ out_w.T
        key = jax.random.key(seed)
        ks = jax.random.split(key, 20)
        B, L = (8, 128)
        s_d = 1.0 / np.sqrt(D_MODEL)
        s_t = 1.0 / np.sqrt(D_T)
        s_h = 1.0 / np.sqrt(HIDDEN)
        return {'x': jax.random.normal(ks[0], (B, L, D_MODEL), jnp.float32), 't': jax.random.normal(ks[1], (B, D_T), jnp.float32), 'Wq': jax.random.normal(ks[2], (D_MODEL, D_MODEL), jnp.float32) * s_d, 'Wk': jax.random.normal(ks[3], (D_MODEL, D_MODEL), jnp.float32) * s_d, 'Wv': jax.random.normal(ks[4], (D_MODEL, D_MODEL), jnp.float32) * s_d, 'Wo': jax.random.normal(ks[5], (D_MODEL, D_MODEL), jnp.float32) * s_d, 'g1w': jax.random.normal(ks[6], (D_MODEL, D_T), jnp.float32) * s_t, 'g1b': jnp.ones((D_MODEL,), jnp.float32), 'b1w': jax.random.normal(ks[7], (D_MODEL, D_T), jnp.float32) * s_t, 'b1b': jnp.zeros((D_MODEL,), jnp.float32), 'g2w': jax.random.normal(ks[8], (D_MODEL, D_T), jnp.float32) * s_t, 'g2b': jnp.ones((D_MODEL,), jnp.float32), 'b2w': jax.random.normal(ks[9], (D_MODEL, D_T), jnp.float32) * s_t, 'b2b': jnp.zeros((D_MODEL,), jnp.float32), 'gate_w': jax.random.normal(ks[10], (HIDDEN, D_MODEL), jnp.float32) * s_d, 'hid_w': jax.random.normal(ks[11], (HIDDEN, D_MODEL), jnp.float32) * s_d, 'out_w': jax.random.normal(ks[12], (D_MODEL, HIDDEN), jnp.float32) * s_h}
    _L0_cond_all = _L0_cond_setup()
    _L0_cond_in = {k: v for k, v in _L0_cond_all.items() if k in ('Wq', 'Wk', 'Wv', 'Wo', 'g1w', 'g1b', 'b1w', 'b1b', 'g2w', 'g2b', 'b2w', 'b2b', 'gate_w', 'hid_w', 'out_w')}
    del _L0_cond_all
    return {'x': x, 'cond_256': cond_256, 'L0_cond_Wq': _L0_cond_in['Wq'], 'L0_cond_Wk': _L0_cond_in['Wk'], 'L0_cond_Wv': _L0_cond_in['Wv'], 'L0_cond_Wo': _L0_cond_in['Wo'], 'L0_cond_g1w': _L0_cond_in['g1w'], 'L0_cond_g1b': _L0_cond_in['g1b'], 'L0_cond_b1w': _L0_cond_in['b1w'], 'L0_cond_b1b': _L0_cond_in['b1b'], 'L0_cond_g2w': _L0_cond_in['g2w'], 'L0_cond_g2b': _L0_cond_in['g2b'], 'L0_cond_b2w': _L0_cond_in['b2w'], 'L0_cond_b2b': _L0_cond_in['b2b'], 'L0_cond_gate_w': _L0_cond_in['gate_w'], 'L0_cond_hid_w': _L0_cond_in['hid_w'], 'L0_cond_out_w': _L0_cond_in['out_w']}

def reference(x, cond_256, L0_cond_Wq, L0_cond_Wk, L0_cond_Wv, L0_cond_Wo, L0_cond_g1w, L0_cond_g1b, L0_cond_b1w, L0_cond_b1b, L0_cond_g2w, L0_cond_g2b, L0_cond_b2w, L0_cond_b2b, L0_cond_gate_w, L0_cond_hid_w, L0_cond_out_w):
    import jax
    import jax.numpy as jnp

    def _L0_cond_ref(x, t, Wq, Wk, Wv, Wo, g1w, g1b, b1w, b1b, g2w, g2b, b2w, b2b, gate_w, hid_w, out_w):
        import jax, jax.numpy as jnp
        import numpy as np
        D_MODEL = 128
        D_T = 32
        N_HEADS = 16
        HIDDEN = 4 * D_MODEL
        EPS = 1e-06

        def _tc_rmsnorm(x, t, gw, gb, bw, bb):
            g = (t @ gw.T + gb)[:, None, :]
            b = (t @ bw.T + bb)[:, None, :]
            inv_rms = jax.lax.rsqrt(jnp.mean(x * x, axis=-1, keepdims=True) + EPS)
            return g * x * inv_rms + b

        def _attention(x, Wq, Wk, Wv, Wo):
            B, L, D = x.shape
            H = N_HEADS
            dh = D // H
            scale = np.sqrt(dh).astype(np.float32)
            q = (x @ Wq.T).reshape(B, L, H, dh)
            k = (x @ Wk.T).reshape(B, L, H, dh)
            v = (x @ Wv.T).reshape(B, L, H, dh)
            attn = jnp.einsum('blhd,bmhd->bhlm', q, k) / scale
            p = jax.nn.softmax(attn, axis=-1)
            o = jnp.einsum('bhlm,bmhd->blhd', p, v).reshape(B, L, D)
            return o @ Wo.T

        def _swiglu(x, gate_w, hid_w, out_w):
            return jax.nn.silu(x @ gate_w.T) * (x @ hid_w.T) @ out_w.T
        x = x + _attention(_tc_rmsnorm(x, t, g1w, g1b, b1w, b1b), Wq, Wk, Wv, Wo)
        return x + _swiglu(_tc_rmsnorm(x, t, g2w, g2b, b2w, b2b), gate_w, hid_w, out_w)
    x = x + _L0_cond_ref(x, cond_256, L0_cond_Wq, L0_cond_Wk, L0_cond_Wv, L0_cond_Wo, L0_cond_g1w, L0_cond_g1b, L0_cond_b1w, L0_cond_b1b, L0_cond_g2w, L0_cond_g2b, L0_cond_b2w, L0_cond_b2b, L0_cond_gate_w, L0_cond_hid_w, L0_cond_out_w)
    return x

_drawn_inputs = setup_inputs


def setup_inputs(seed=0):
    import zlib

    import numpy as np

    out = dict(_drawn_inputs(seed))
    spreads = {'L0_cond_g1b': (1.0, 0.2),
     'L0_cond_b1b': (0.0, 0.1),
     'L0_cond_g2b': (1.0, 0.2),
     'L0_cond_b2b': (0.0, 0.1)}
    factors = {}
    for name, (base, spread) in spreads.items():
        noise = np.random.default_rng([zlib.crc32(name.encode()), seed]).standard_normal(out[name].shape)
        drawn = base * np.exp(spread * noise) if base else spread * noise
        out[name] = jnp.asarray(drawn.astype(out[name].dtype))
    for name, factor in factors.items():
        out[name] = (out[name] * factor).astype(out[name].dtype)
    return out
```

```python
from contextlib import ExitStack

import concourse.bass as bass
from concourse import mybir

ALU = mybir.AluOpType
ACT = mybir.ActivationFunctionType
AX = mybir.AxisListType
F32 = mybir.dt.float32
F32R = mybir.dt.float32r
BF16 = mybir.dt.bfloat16

EPS = 1e-6


def bass_cond_transformer_block(
    nc: bass.Bass,
    x: bass.AP,
    cond: bass.AP,
    mod_w: bass.AP,
    mod_b: bass.AP,
    attn_w: bass.AP,
    ffn_in_w: bass.AP,
    ffn_out_w: bass.AP,
    out: bass.AP,
):
    L, B, D = x.shape
    DT = cond.shape[0]
    H = 16
    DH = D // H
    HC = ffn_out_w.shape[1]
    NB = 4
    G = B // NB
    W = NB * L
    HQ = 4
    CH = H // HQ
    NK = NB * CH
    NP = 4
    VW = 32
    PARTS = 3
    Q_PART = [0, 0, 0, 1, 1, 2]
    K_PART = [0, 1, 2, 0, 1, 0]
    ROWS = DH * len(Q_PART)
    ROWS_MAX = ROWS + 2
    STK = 16 * 2 * len(Q_PART)
    SCALE = float(DH) ** -0.5
    assert D == 128 and L == 128 and W == 512 and B % (2 * NB) == 0 and H * DH == D and HC == 4

    PV_LAG = 2
    RAW_LAG = 4
    OTS, TR4, TRO, WO, XS2, XT2 = 5, 7, 8, 9, 11, 14
    MS_SLOT, XS_SLOT = 5, 9
    XT_SLOT, V_SLOT, CT_SLOT, Q_SLOT, K_SLOT, FFN_SLOT = 12, 17, 21, 22, 23, 27
    LAST_SLOT = FFN_SLOT + HC

    ctx = ExitStack()
    with ctx:
        def sb(name, shape, dt=F32):
            return ctx.enter_context(nc.sbuf_tensor(name, shape, dt))

        def bank(name):
            return ctx.enter_context(nc.psum_tensor(name, [128, 512], F32))

        def sem(name):
            return ctx.enter_context(nc.semaphore(name))

        cond_s = sb("cond_s", [DT, B])
        mod_w_s = sb("mod_w_s", [DT, 4, D])
        mod_b_s = sb("mod_b_s", [D, 4])
        attn_w_s = sb("attn_w_s", [D, 4, D])
        ffn_in_s = sb("ffn_in_s", [D, 2, HC * 128])
        ffn_out_s = sb("ffn_out_s", [128, HC, D])
        qk_hi = sb("qk_hi", [D, 2, D], F32R)
        qk_lo = sb("qk_lo", [D, 2, D], F32R)
        ffn_hi = sb("ffn_hi", [D, 2, HC * 128], F32R)
        ffn_lo = sb("ffn_lo", [D, 2, HC * 128], F32R)
        mod = sb("mod", [D, 4, B])
        ident = sb("ident", [128, 128])
        mhalf = sb("mhalf", [128, NB])
        ones = sb("ones", [H * NB, L], BF16)
        x_s = sb("x_s", [L, B * D])
        sqx = sb("sqx", [L, NB, D])
        sq1 = sb("sq1", [L, NB])
        ms1 = sb("ms1", [L, NB])
        inv1 = sb("inv1", [L, NB])
        xs1 = sb("xs1", [L, NB, D])
        xn1 = sb("xn1", [D, NB, L])
        xn1_hi = sb("xn1_hi", [D, W], F32R)
        xn1_lo = sb("xn1_lo", [D, W], F32R)
        qp = sb("qp", [D, PARTS, W], BF16)
        kp = sb("kp", [D, PARTS, W], BF16)
        q_rest = sb("q_rest", [D, W])
        k_rest = sb("k_rest", [D, W])
        qs = [sb(f"qs{u}", [64, H, W], BF16) for u in range(2)]
        ks = [sb(f"ks{u}", [64, H, W], BF16) for u in range(2)]
        va = [sb(f"va{u}", [L, NB, H, VW]) for u in range(2)]
        nmax = sb("nmax", [L, 128])
        shift = sb("shift", [H * NB, 2, L], BF16)
        p_s = sb("p_s", [L, NP, HQ * L])
        ot_s = sb("ot_s", [128, 2, CH * L])
        rden = sb("rden", [L, H])
        o_s = sb("o_s", [L, D])
        oT_s = sb("oT_s", [D, L])
        x1 = sb("x1", [L, NB, D])
        sqx1 = sb("sqx1", [L, NB, D])
        ms2 = sb("ms2", [L, NB])
        inv2 = sb("inv2", [L, NB])
        xs2 = sb("xs2", [L, NB, D])
        xn2 = sb("xn2", [D, NB, L])
        xn2_hi = sb("xn2_hi", [D, NB, L], F32R)
        xn2_lo = sb("xn2_lo", [D, NB, L], F32R)
        th = sb("th", [128, 2, W])
        gated = sb("gated", [128, W])
        hT = sb("hT", [128, 2, W])
        resid = sb("resid", [L, W])

        score = [bank("score0"), bank("score1")]
        gate_up = [bank("gate"), bank("up")]
        pv = [bank("pv0"), bank("pv1")]
        ffn_y = pv[1]
        tok = bank("tok")
        small = bank("small")

        s_x = [sem("s_xin0"), sem("s_xin1")]
        s_modw, s_attnw, s_ffnin, s_ffnout = sem("s_modw"), sem("s_attnw"), sem("s_ffnin"), sem("s_ffnout")
        s_stack = [sem("s_stack0"), sem("s_stack1")]
        s_shiftrow = [sem("s_shiftrow0"), sem("s_shiftrow1")]
        s_out = sem("s_out")
        s_ident0, s_ident, s_mhalf, s_va0, s_ones = (sem("s_ident0"), sem("s_ident"), sem("s_mhalf"), sem("s_va0"),
                                                     sem("s_ones"))
        s_onerows = sem("s_onerows")
        s_modp, s_mod, s_whi, s_wlo = sem("s_modp"), sem("s_mod"), sem("s_whi"), sem("s_wlo")
        s_sq1 = sem("s_sq1")
        s_ms1, s_inv1, s_xs1, s_xt1, s_xn1, s_hi1, s_lo1 = (sem("s_ms1"), sem("s_inv1"), sem("s_xs1"), sem("s_xt1"),
                                                            sem("s_xn1"), sem("s_hi1"), sem("s_lo1"))
        s_v, s_va = sem("s_v"), sem("s_va")
        s_q, s_qhi, s_qrest, s_qmid, s_qlo = sem("s_q"), sem("s_qhi"), sem("s_qrest"), sem("s_qmid"), sem("s_qlo")
        s_k, s_khi, s_krest, s_kmid, s_klo = sem("s_k"), sem("s_khi"), sem("s_krest"), sem("s_kmid"), sem("s_klo")
        s_raw, s_max, s_maxT, s_shi, s_slo = sem("s_raw"), sem("s_max"), sem("s_maxT"), sem("s_shi"), sem("s_slo")
        s_score, s_exp, s_pv, s_ot, s_tr4, s_rden = (sem("s_score"), sem("s_exp"), sem("s_pv"), sem("s_ot"),
                                                     sem("s_tr4"), sem("s_rden"))
        s_o, s_oTp, s_oT, s_wo, s_x1 = sem("s_o"), sem("s_oTp"), sem("s_oT"), sem("s_wo"), sem("s_x1")
        s_ms2, s_inv2, s_xs2, s_xt2, s_xn2, s_hi2, s_lo2 = (sem("s_ms2"), sem("s_inv2"), sem("s_xs2"), sem("s_xt2"),
                                                            sem("s_xn2"), sem("s_hi2"), sem("s_lo2"))
        s_gate, s_up, s_tanh, s_gated, s_h, s_y, s_resid, s_fin = (
            sem("s_gate"), sem("s_up"), sem("s_tanh"), sem("s_gated"), sem("s_h"), sem("s_y"), sem("s_resid"),
            sem("s_fin"))

        def num(g):
            return g[0] * 2 + g[1]

        def plus(g, n):
            return (g[0] + (g[1] + n) // 2, (g[1] + n) % 2)

        def cols(g):
            return bass.ds(num(g) * W, W)

        def run_steps(eng, step):
            step(None, None, (0, 0))
            step(None, (0, 0), (0, 1))
            step((0, 0), (0, 1), (1, 0))
            step((0, 1), (1, 0), (1, 1))
            with eng.Fori(1, G // 2 - 1) as i:
                for u in range(2):
                    step((i, u), plus((i, u), 1), plus((i, u), 2))
            step((G // 2 - 1, 0), (G // 2 - 1, 1), None)
            step((G // 2 - 1, 1), None, None)

        block = ctx.enter_context(nc.Block())

        @block.sync
        def _(sp):
            def ahead(value):
                return value if isinstance(value, int) else sp.compute_val(value)

            def load_x(g, loaded, at):
                sp.wait_ge(s_x[g[1]], loaded)
                sp.dma_start(x_s[:, bass.ds(at, W)],
                             x.rearrange("l b d -> l (b d)")[:, bass.ds(at, W)]).then_inc(s_x[g[1]], 16)

            def stack_rows(g, n, dst, parts, part_of, part, ready):
                sp.wait_ge(ready, n)
                for r in range(len(part_of)):
                    if part_of[r] == part:
                        sp.dma_start(dst[g[1]][DH * r:DH * r + DH, :, :].rearrange("d h w -> d (h w)"),
                                     parts[:, part, :]).then_inc(s_stack[g[1]], 16)

            def step(c, b, a):
                if c is not None:
                    c_at = ahead(num(c) * W)
                    c_done = ahead(num(c) + 1)
                    scores_before, scores_done = ahead(NK * num(c)), ahead(NK * (num(c) + 1))
                if b is not None:
                    b_done = ahead(num(b) + 1)
                if a is not None:
                    a_at, a_loaded, a_done = ahead(num(a) * W), ahead(a[0] * 16), ahead(num(a) + 1)
                if c is not None and a is not None:
                    load_x(a, a_loaded, a_at)
                if b is not None:
                    if c is not None:
                        sp.wait_ge(s_score, scores_before)
                    sp.wait_ge(s_shi, b_done)
                    sp.dma_start(qs[b[1]][ROWS:ROWS + 1, :, :].rearrange("d h w -> d (h w)"),
                                 shift[:, 0, :]).then_inc(s_shiftrow[b[1]], 16)
                    sp.wait_ge(s_slo, b_done)
                    sp.dma_start(qs[b[1]][ROWS + 1:ROWS + 2, :, :].rearrange("d h w -> d (h w)"),
                                 shift[:, 1, :]).then_inc(s_shiftrow[b[1]], 16)
                if a is not None:
                    if c is not None:
                        sp.wait_ge(s_score, scores_done)
                    stack_rows(a, a_done, qs, qp, Q_PART, 0, s_qhi)
                    stack_rows(a, a_done, qs, qp, Q_PART, 1, s_qmid)
                    stack_rows(a, a_done, ks, kp, K_PART, 0, s_khi)
                    stack_rows(a, a_done, ks, kp, K_PART, 1, s_kmid)
                    stack_rows(a, a_done, qs, qp, Q_PART, 2, s_qlo)
                    stack_rows(a, a_done, ks, kp, K_PART, 2, s_klo)
                if c is not None:
                    sp.wait_ge(s_fin, c_done)
                    sp.dma_start(out.rearrange("l b d -> l (b d)")[:, bass.ds(c_at, W)],
                                 x_s[:, bass.ds(c_at, W)]).then_inc(s_out, 16)

            load_x((0, 0), 0, 0)
            sp.dma_start(attn_w_s[:], attn_w).then_inc(s_attnw, 16)
            load_x((0, 1), 0, W)
            sp.dma_start(ffn_in_s[:], ffn_in_w).then_inc(s_ffnin, 16)
            sp.dma_start(ffn_out_s[:], ffn_out_w).then_inc(s_ffnout, 16)

            run_steps(sp, step)
            sp.wait_ge(s_out, 16 * G)

        @block.tensor
        def _(pe):
            def split_product(dst, w_hi, w_lo, v_hi, v_lo):
                pe.matmul(dst, w_hi, v_hi, start=True, stop=False)
                pe.matmul(dst, w_hi, v_lo, start=False, stop=False)
                return pe.matmul(dst, w_lo, v_hi, start=False, stop=True)

            def a_transpose(g, c):
                pe.wait_ge(s_xs1, num(g) + 1)
                if c is not None:
                    pe.wait_ge(s_o, NB * num(c) + 2)
                else:
                    pe.wait_ge(s_va, num(g))
                for b in range(NB):
                    mm = pe.transpose(tok[:, b * L:(b + 1) * L], xs1[:, b, :], ident[:])
                mm.then_inc(s_xt1, 1)

            def a_values(g, c):
                pe.wait_ge(s_xn1, NB * (num(g) + 1))
                if c is not None:
                    pe.wait_ge(s_o, NB * num(c) + 3)
                for b in range(NB):
                    mm = pe.matmul(tok[:, b * L:(b + 1) * L], xn1[:, b, :], attn_w_s[:, 2, :], start=True, stop=True)
                mm.then_inc(s_v, 1)

            def a_query(g, c):
                if c is not None:
                    pe.wait_ge(s_exp, NK * (num(c) + 1) - 1)
                else:
                    pe.wait_ge(s_qrest, num(g))
                pe.wait_ge(s_lo1, num(g) + 1)
                split_product(score[0][:], qk_hi[:, 0, :], qk_lo[:, 0, :], xn1_hi[:], xn1_lo[:]).then_inc(s_q, 1)

            def a_key(g, c):
                if c is not None:
                    pe.wait_ge(s_exp, NK * (num(c) + 1))
                else:
                    pe.wait_ge(s_krest, num(g))
                split_product(score[1][:], qk_hi[:, 1, :], qk_lo[:, 1, :], xn1_hi[:], xn1_lo[:]).then_inc(s_k, 1)

            def b_raw(g, c, k):
                b, ch = k // CH, k % CH
                if k == 0:
                    pe.wait_ge(s_stack[g[1]], STK * (g[0] + 1))
                    if c is not None:
                        pe.wait_ge(s_h, HC * num(c))
                if k >= 2:
                    pe.wait_ge(s_max, NK * num(g) + k - 1)
                for j in range(HQ):
                    h = ch * HQ + j
                    mm = pe.matmul(gate_up[k % 2][:, j * L:(j + 1) * L], qs[g[1]][0:ROWS, h, b * L:(b + 1) * L],
                                   ks[g[1]][0:ROWS, h, b * L:(b + 1) * L], start=True, stop=True)
                mm.then_inc(s_raw, 1)

            def b_maxT(g):
                pe.wait_ge(s_max, NK * (num(g) + 1))
                pe.transpose(gate_up[0][:, 0:L], nmax[:], ident[:]).then_inc(s_maxT, 1)

            def c_scores(g, k, first_a):
                b, ch = k // CH, k % CH
                if k == 0:
                    pe.wait_ge(s_shiftrow[g[1]], 32 * (g[0] + 1))
                    pe.wait_ge(s_exp, NK * num(g))
                    if first_a is not None:
                        pe.wait_ge(s_qrest, num(first_a))
                        pe.wait_ge(s_krest, num(first_a))
                if k >= 2:
                    pe.wait_ge(s_exp, NK * num(g) + k - 1)
                for j in range(HQ):
                    h = ch * HQ + j
                    mm = pe.matmul(score[k % 2][:, j * L:(j + 1) * L], ks[g[1]][0:ROWS_MAX, h, b * L:(b + 1) * L],
                                   qs[g[1]][0:ROWS_MAX, h, b * L:(b + 1) * L], start=True, stop=True)
                mm.then_inc(s_score, 1)

            def c_pv(g, k):
                b, ch = k // CH, k % CH
                if k == 0:
                    pe.wait_ge(s_va, num(g) + 1)
                    pe.wait_ge(s_ot, NB * num(g))
                    pe.wait_ge(s_fin, num(g))
                if ch == 0 and b >= 2:
                    pe.wait_ge(s_ot, NB * num(g) + b - 1)
                pe.wait_ge(s_exp, NK * num(g) + k + 1)
                for j in range(HQ):
                    h = ch * HQ + j
                    mm = pe.matmul(pv[b % 2][VW * j:VW * j + VW, ch * L:(ch + 1) * L], va[g[1]][:, b, h, :],
                                   p_s[:, k % NP, j * L:(j + 1) * L], start=True, stop=True)
                mm.then_inc(s_pv, 1)

            def c_tr4(g, b, a):
                pe.wait_ge(s_ot, NB * num(g) + b + 1)
                pe.wait_ge(s_o, NB * num(g) + b)
                if b == 0 and a is not None:
                    pe.wait_ge(s_va, num(a))
                if b == 2 and a is not None:
                    pe.wait_ge(s_xn1, NB * (num(a) + 1))
                if b == 3 and a is not None:
                    pe.wait_ge(s_va, num(a) + 1)
                for ch in range(CH):
                    mm = pe.transpose(tok[:, ch * 128:(ch + 1) * 128], ot_s[:, b % 2, ch * L:(ch + 1) * L], ident[:])
                mm.then_inc(s_tr4, 1)

            def c_tro(g, b):
                pe.wait_ge(s_o, NB * num(g) + b + 1)
                if b >= 2:
                    pe.wait_ge(s_xn2, NB * num(g) + b - 1)
                else:
                    pe.wait_ge(s_xn2, NB * num(g))
                    if b == 1:
                        pe.wait_ge(s_x1, NB * num(g) + 1)
                pe.transpose(small[:, 0:L], o_s[:], ident[:]).then_inc(s_oTp, 1)

            def c_wo(g, b):
                pe.wait_ge(s_oT, NB * num(g) + b + 1)
                pe.matmul(small[:, L:2 * L], oT_s[:], attn_w_s[:, 3, :], start=True, stop=True).then_inc(s_wo, 1)

            def d_xt2(g, b):
                pe.wait_ge(s_xs2, NB * num(g) + b + 1)
                pe.wait_ge(s_x1, NB * num(g) + min(b + 2, NB))
                pe.transpose(small[:, 2 * L:3 * L], xs2[:, b, :], ident[:]).then_inc(s_xt2, 1)

            def d_gate_up(g, ch, b):
                if ch == 0:
                    pe.wait_ge(s_lo2, NB * (num(g) + 1))
                    if b is not None:
                        pe.wait_ge(s_slo, num(b) + 1)
                        pe.wait_ge(s_max, NK * (num(b) + 1))
                else:
                    pe.wait_ge(s_gated, HC * num(g) + ch)
                cs = slice(ch * 128, ch * 128 + 128)
                hi, lo = xn2_hi[:].rearrange("d b l -> d (b l)"), xn2_lo[:].rearrange("d b l -> d (b l)")
                split_product(gate_up[0][:], ffn_hi[:, 0, cs], ffn_lo[:, 0, cs], hi, lo).then_inc(s_gate, 1)
                if ch > 0:
                    pe.wait_ge(s_h, HC * num(g) + ch)
                split_product(gate_up[1][:], ffn_hi[:, 1, cs], ffn_lo[:, 1, cs], hi, lo).then_inc(s_up, 1)

            def d_out(g, ch):
                if ch == 0:
                    pe.wait_ge(s_ot, NB * (num(g) + 1))
                pe.wait_ge(s_h, HC * num(g) + ch + 1)
                for b in range(NB):
                    mm = pe.matmul(ffn_y[:, b * D:(b + 1) * D], hT[:, ch % 2, b * L:(b + 1) * L], ffn_out_s[:, ch, :],
                                   start=(ch == 0 and b == 0), stop=(ch == HC - 1), skip_group_check=True)
                mm.then_inc(s_y, 1)

            def step(c, b, a):
                first_a = plus(c, 2) if c is not None and a is not None else ((G // 2, 0) if c is not None else None)
                for s in range(LAST_SLOT + 1):
                    if c is not None:
                        if s < NK:
                            c_scores(c, s, first_a)
                        if 0 <= s - PV_LAG < NK:
                            c_pv(c, s - PV_LAG)
                    if b is not None and 0 <= s - RAW_LAG < NK:
                        b_raw(b, c, s - RAW_LAG)
                    if a is not None and s == XT_SLOT:
                        a_transpose(a, c)
                    if a is not None and s == V_SLOT:
                        a_values(a, c)
                    for n in range(NB if c is not None else 0):
                        if s == 4 * n + TR4:
                            c_tr4(c, n, a)
                        if s == 4 * n + TRO:
                            c_tro(c, n)
                        if s == 4 * n + WO:
                            c_wo(c, n)
                        if s == 4 * n + XT2:
                            d_xt2(c, n)
                    if b is not None and s == CT_SLOT:
                        b_maxT(b)
                    if a is not None and s == Q_SLOT:
                        a_query(a, c)
                    if a is not None and s == K_SLOT:
                        a_key(a, c)
                    if c is not None and 0 <= s - FFN_SLOT < HC:
                        d_gate_up(c, s - FFN_SLOT, b)
                    if c is not None and 0 <= s - FFN_SLOT - 1 < HC:
                        d_out(c, s - FFN_SLOT - 1)

            pe.wait_ge(s_modw, 48)
            for i in range(4):
                mm = pe.matmul(small[:, i * B:(i + 1) * B], mod_w_s[:, i, :], cond_s[:], start=True, stop=True)
            mm.then_inc(s_modp, 1)
            pe.wait_ge(s_ident, 1)
            pe.wait_ge(s_attnw, 16)
            pe.wait_ge(s_ffnout, 16)
            pe.wait_ge(s_wlo, 2)
            pe.wait_ge(s_onerows, 64)
            run_steps(pe, step)

        @block.scalar
        def _(act):
            def a_norm(g, c):
                act.wait_ge(s_xt1, num(g) + 1)
                act.wait_ge(s_v, num(g))
                act.wait_ge(s_lo1, num(g))
                for b in range(NB):
                    act.activation(xn1[:, b, :], tok[:, b * L:(b + 1) * L], ACT.Identity,
                                   scale=mod[:, 0, bass.ds(num(g) * NB + b, 1)],
                                   bias=mod[:, 1, bass.ds(num(g) * NB + b, 1)]).then_inc(s_xn1, 1)

            def a_values(g, c):
                act.wait_ge(s_v, num(g) + 1)
                if c is not None:
                    act.wait_ge(s_pv, NK * (num(c) + 1))
                act.activation(va[g[1]][:, :, :, 0:DH].rearrange("l b h d -> l (b h) d"),
                               tok[:].rearrange("l (n d) -> l n d", d=DH), ACT.Copy).then_inc(s_va, 1)

            def a_high(g, ready, src, dst, done):
                act.wait_ge(ready, num(g) + 1)
                before = plus(g, -1)
                if not (isinstance(g[0], int) and num(g) == 0):
                    act.wait_ge(s_stack[before[1]], STK * (before[0] + 1))
                act.activation(dst[:, 0, :], src[:], ACT.Copy).then_inc(done, 1)

            def c_exp(g, k):
                act.wait_ge(s_score, NK * num(g) + k + 1)
                if k == 0:
                    act.wait_ge(s_pv, NK * num(g))
                if k >= NP:
                    act.wait_ge(s_pv, NK * num(g) + k - NP + 1)
                act.activation(p_s[:, k % NP, :], score[k % 2][:], ACT.Exp, scale=SCALE).then_inc(s_exp, 1)

            def c_ot(g, b):
                act.wait_ge(s_pv, NK * num(g) + CH * (b + 1))
                if b >= 2:
                    act.wait_ge(s_tr4, NB * num(g) + b - 1)
                else:
                    act.wait_ge(s_tr4, NB * num(g))
                act.activation(ot_s[:, b % 2, :], pv[b % 2][:], ACT.Copy).then_inc(s_ot, 1)

            def c_oT(g, b):
                act.wait_ge(s_oTp, NB * num(g) + b + 1)
                act.wait_ge(s_wo, NB * num(g) + b)
                act.activation(oT_s[:], small[:, 0:L], ACT.Copy).then_inc(s_oT, 1)

            def d_norm(g, b):
                act.wait_ge(s_xt2, NB * num(g) + b + 1)
                act.wait_ge(s_lo2, NB * num(g))
                act.activation(xn2[:, b, :], small[:, 2 * L:3 * L], ACT.Identity,
                               scale=mod[:, 2, bass.ds(num(g) * NB + b, 1)],
                               bias=mod[:, 3, bass.ds(num(g) * NB + b, 1)]).then_inc(s_xn2, 1)

            def d_tanh(g, ch):
                act.wait_ge(s_gate, HC * num(g) + ch + 1)
                if ch < 2:
                    act.wait_ge(s_gated, HC * num(g))
                else:
                    act.wait_ge(s_gated, HC * num(g) + ch - 1)
                act.activation(th[:, ch % 2, :], gate_up[0][:], ACT.Tanh, scale=0.5).then_inc(s_tanh, 1)

            def step(c, b, a):
                for s in range(LAST_SLOT + 1):
                    if c is not None and s < NK:
                        c_exp(c, s)
                    if a is not None and s == XT_SLOT:
                        a_norm(a, c)
                    if a is not None and s == V_SLOT:
                        a_values(a, c)
                    for n in range(NB if c is not None else 0):
                        if s == 4 * n + OTS:
                            c_ot(c, n)
                        if s == 4 * n + TRO:
                            c_oT(c, n)
                        if s == 4 * n + XT2:
                            d_norm(c, n)
                    if a is not None and s == Q_SLOT:
                        a_high(a, s_q, score[0], qp, s_qhi)
                    if a is not None and s == K_SLOT:
                        a_high(a, s_k, score[1], kp, s_khi)
                    if c is not None and 0 <= s - FFN_SLOT < HC:
                        d_tanh(c, s - FFN_SLOT)

            act.dma_start(mod_w_s[:], mod_w).then_inc(s_modw, 16)
            act.dma_start(cond_s[:], cond).then_inc(s_modw, 16)
            act.dma_start(mod_b_s[:], mod_b).then_inc(s_modw, 16)
            act.wait_ge(s_ones, 1)
            for u in range(2):
                for row in (ROWS, ROWS + 1):
                    act.dma_start(ks[u][row:row + 1, :, :].rearrange("d h w -> d (h w)"), ones[:]).then_inc(s_onerows, 16)
            act.wait_ge(s_mod, 4)
            act.wait_ge(s_va0, 4)
            run_steps(act, step)

        @block.vector
        def _(dve):
            def a_mean(g):
                dve.wait_ge(s_x[g[1]], 16 * (g[0] + 1))
                dve.wait_ge(s_ms1, num(g))
                for b in range(NB):
                    xb = x_s[:, bass.ds(num(g) * W + b * D, D)]
                    dve.scalar_tensor_tensor(out=sqx[:, b, :], in0=xb, scalar=1.0 / D, in1=xb, op0=ALU.mult, op1=ALU.mult,
                                             accum_out=sq1[:, b:b + 1]).then_inc(s_sq1, 1)
                dve.wait_ge(s_sq1, NB * (num(g) + 1))
                dve.tensor_scalar(ms1[:], sq1[:], EPS, None, ALU.add).then_inc(s_ms1, 1)

            def a_scale(g):
                dve.wait_ge(s_inv1, num(g) + 1)
                dve.wait_ge(s_xt1, num(g))
                dve.tensor_tensor(xs1[:], x_s[:, cols(g)].rearrange("l (b d) -> l b d", b=NB),
                                  inv1[:].unsqueeze(2).to_broadcast([L, NB, D]), ALU.mult).then_inc(s_xs1, 1)

            def a_hi(g):
                dve.wait_ge(s_xn1, NB * (num(g) + 1))
                dve.wait_ge(s_k, num(g))
                dve.wait_ge(s_lo1, num(g))
                dve.tensor_copy(xn1_hi[:], xn1[:].rearrange("d b l -> d (b l)")).then_inc(s_hi1, 1)

            def a_rest(g, src, parts, rest, high, lowest, done, mid):
                dve.wait_ge(high, num(g) + 1)
                dve.wait_ge(lowest, num(g))
                dve.tensor_tensor(rest[:], src[:], parts[:, 0, :], ALU.subtract).then_inc(done, 1)
                dve.wait_ge(done, num(g) + 1)
                dve.tensor_copy(parts[:, 1, :], rest[:]).then_inc(mid, 1)

            def b_max(g, k):
                b, ch = k // CH, k % CH
                dve.wait_ge(s_raw, NK * num(g) + k + 1)
                if k == 0:
                    dve.wait_ge(s_maxT, num(g))
                heads = nmax[:, ch * HQ * NB:(ch + 1) * HQ * NB].rearrange("l (j b) -> l j b", b=NB)
                dve.tensor_reduce(heads[:, :, b], gate_up[k % 2][:].rearrange("l (j m) -> l j m", j=HQ),
                                  AX.X, ALU.max, negate=True).then_inc(s_max, 1)

            def b_shift(g):
                dve.wait_ge(s_maxT, num(g) + 1)
                before = plus(g, -1)
                if not (isinstance(g[0], int) and num(g) == 0):
                    dve.wait_ge(s_shiftrow[before[1]], 32 * (before[0] + 1))
                dve.tensor_copy(shift[:, 0, :], gate_up[0][0:H * NB, 0:L]).then_inc(s_shi, 1)
                dve.wait_ge(s_shi, num(g) + 1)
                dve.tensor_tensor(shift[:, 1, :], gate_up[0][0:H * NB, 0:L], shift[:, 0, :],
                                  ALU.subtract).then_inc(s_slo, 1)

            def c_norm(g, b):
                dve.wait_ge(s_tr4, NB * num(g) + b + 1)
                heads = tok[:].rearrange("l (h v) -> l h v", v=VW)
                dve.reciprocal(rden[:], heads[:, :, DH]).then_inc(s_rden, 1)
                dve.wait_ge(s_rden, NB * num(g) + b + 1)
                dve.wait_ge(s_oTp, NB * num(g) + b)
                dve.tensor_tensor(o_s[:].rearrange("l (h d) -> l h d", h=H), heads[:, :, 0:DH],
                                  rden[:].unsqueeze(2).to_broadcast([L, H, DH]), ALU.mult).then_inc(s_o, 1)

            def c_x1(g, b):
                dve.wait_ge(s_wo, NB * num(g) + b + 1)
                if b == 0:
                    dve.wait_ge(s_resid, num(g))
                dve.tensor_tensor(x1[:, b, :], small[:, L:2 * L], x_s[:, bass.ds(num(g) * W + b * D, D)],
                                  ALU.add).then_inc(s_x1, 1)
                dve.wait_ge(s_x1, NB * num(g) + b + 1)
                dve.wait_ge(s_ms2, NB * num(g))
                dve.tensor_tensor_reduce(sqx1[:, b, :], x1[:, b, :], x1[:, b, :], 1.0 / D, EPS, ALU.mult, ALU.add,
                                         ms2[:, b:b + 1]).then_inc(s_ms2, 1)

            def d_scale(g, b):
                dve.wait_ge(s_inv2, NB * num(g) + b + 1)
                dve.wait_ge(s_xt2, NB * num(g))
                dve.tensor_scalar(xs2[:, b, :], x1[:, b, :], inv2[:, b:b + 1], None, ALU.mult).then_inc(s_xs2, 1)

            def d_hi(g, b):
                dve.wait_ge(s_xn2, NB * num(g) + b + 1)
                if b == 0:
                    dve.wait_ge(s_up, HC * num(g))
                    dve.wait_ge(s_lo2, NB * num(g))
                dve.tensor_copy(xn2_hi[:, b, :], xn2[:, b, :]).then_inc(s_hi2, 1)

            def d_hidden(g, ch):
                dve.wait_ge(s_tanh, HC * num(g) + ch + 1)
                dve.wait_ge(s_h, HC * num(g) + ch)
                dve.scalar_tensor_tensor(out=gated[:], in0=th[:, ch % 2, :], scalar=1.0, in1=gate_up[0][:],
                                         op0=ALU.add, op1=ALU.mult).then_inc(s_gated, 1)
                dve.wait_ge(s_up, HC * num(g) + ch + 1)
                dve.wait_ge(s_gated, HC * num(g) + ch + 1)
                if ch < 2:
                    dve.wait_ge(s_y, HC * num(g))
                else:
                    dve.wait_ge(s_y, HC * num(g) + ch - 1)
                dve.scalar_tensor_tensor(out=hT[:, ch % 2, :], in0=gated[:], scalar=0.5, in1=gate_up[1][:],
                                         op0=ALU.mult, op1=ALU.mult).then_inc(s_h, 1)

            def d_final(g):
                dve.wait_ge(s_y, HC * (num(g) + 1))
                dve.wait_ge(s_resid, num(g) + 1)
                dve.tensor_tensor(x_s[:, cols(g)], ffn_y[:], resid[:], ALU.add).then_inc(s_fin, 1)

            def step(c, b, a):
                for s in range(LAST_SLOT + 1):
                    for n in range(NB if c is not None else 0):
                        if s == 4 * n + TR4:
                            c_norm(c, n)
                        if s == 4 * n + WO:
                            c_x1(c, n)
                        if s == 4 * n + XS2:
                            d_scale(c, n)
                        if s == 4 * n + XT2:
                            d_hi(c, n)
                    if b is not None and 0 <= s - RAW_LAG < NK:
                        b_max(b, s - RAW_LAG)
                    if a is not None and s == MS_SLOT:
                        a_mean(a)
                    if a is not None and s == XS_SLOT:
                        a_scale(a)
                    if a is not None and s == XT_SLOT + 1:
                        a_hi(a)
                    if b is not None and s == CT_SLOT:
                        b_shift(b)
                    if a is not None and s == Q_SLOT:
                        a_rest(a, score[0], qp, q_rest, s_qhi, s_qlo, s_qrest, s_qmid)
                    if a is not None and s == K_SLOT:
                        a_rest(a, score[1], kp, k_rest, s_khi, s_klo, s_krest, s_kmid)
                    if c is not None and 0 <= s - FFN_SLOT < HC:
                        d_hidden(c, s - FFN_SLOT)
                    if c is not None and s == LAST_SLOT:
                        d_final(c)

            dve.memset(ones[:], 1.0).then_inc(s_ones, 1)
            dve.wait_ge(s_modp, 1)
            dve.wait_ge(s_modw, 48)
            for i in range(4):
                dve.tensor_scalar(mod[:, i, :], small[:, i * B:(i + 1) * B], mod_b_s[:, i:i + 1], None,
                                  ALU.add).then_inc(s_mod, 1)
            dve.wait_ge(s_attnw, 16)
            dve.tensor_copy(qk_hi[:], attn_w_s[:, 0:2, :]).then_inc(s_whi, 1)
            dve.wait_ge(s_mhalf, 2)
            dve.wait_ge(s_ffnin, 16)
            dve.tensor_copy(ffn_hi[:], ffn_in_s[:]).then_inc(s_whi, 1)
            run_steps(dve, step)

        @block.gpsimd
        def _(pool):
            def a_inv(g):
                pool.wait_ge(s_ms1, num(g) + 1)
                pool.wait_ge(s_xs1, num(g))
                pool.tensor_tensor(inv1[:], ms1[:], mhalf[:], ALU.pow).then_inc(s_inv1, 1)

            def a_lo(g):
                pool.wait_ge(s_hi1, num(g) + 1)
                pool.wait_ge(s_k, num(g))
                pool.tensor_tensor(xn1_lo[:], xn1[:].rearrange("d b l -> d (b l)"), xn1_hi[:].bitcast(F32),
                                   ALU.subtract).then_inc(s_lo1, 1)

            def a_lowest(g, rest, parts, mid, done):
                pool.wait_ge(mid, num(g) + 1)
                before = plus(g, -1)
                if not (isinstance(g[0], int) and num(g) == 0):
                    pool.wait_ge(s_stack[before[1]], STK * (before[0] + 1))
                pool.tensor_tensor(parts[:, 2, :], rest[:], parts[:, 1, :], ALU.subtract).then_inc(done, 1)

            def d_inv(g, b):
                pool.wait_ge(s_ms2, NB * num(g) + b + 1)
                pool.wait_ge(s_xs2, NB * num(g))
                pool.tensor_tensor(inv2[:, b:b + 1], ms2[:, b:b + 1], mhalf[:, 0:1], ALU.pow).then_inc(s_inv2, 1)

            def d_lo(g, b):
                pool.wait_ge(s_hi2, NB * num(g) + b + 1)
                if b == 0:
                    pool.wait_ge(s_up, HC * num(g))
                pool.tensor_tensor(xn2_lo[:, b, :], xn2[:, b, :], xn2_hi[:, b, :].bitcast(F32),
                                   ALU.subtract).then_inc(s_lo2, 1)

            def d_resid(g):
                pool.wait_ge(s_x1, NB * (num(g) + 1))
                pool.wait_ge(s_fin, num(g))
                pool.tensor_tensor(resid[:], x1[:].rearrange("l b d -> l (b d)"), x_s[:, cols(g)],
                                   ALU.add).then_inc(s_resid, 1)

            def step(c, b, a):
                for s in range(LAST_SLOT + 1):
                    for n in range(NB if c is not None else 0):
                        if s == 4 * n + WO:
                            d_inv(c, n)
                        if s == 4 * n + XT2:
                            d_lo(c, n)
                    if a is not None and s == MS_SLOT:
                        a_inv(a)
                    if a is not None and s == XT_SLOT + 1:
                        a_lo(a)
                    if a is not None and s == Q_SLOT:
                        a_lowest(a, q_rest, qp, s_qmid, s_qlo)
                    if a is not None and s == K_SLOT:
                        a_lowest(a, k_rest, kp, s_kmid, s_klo)
                    if c is not None and s == FFN_SLOT:
                        d_resid(c)

            pool.memset(ident[:], 0.0).then_inc(s_ident0, 1)
            pool.memset(mhalf[:], -0.5).then_inc(s_mhalf, 1)
            pool.memset(nmax[:], 0.0).then_inc(s_mhalf, 1)
            pool.wait_ge(s_ident0, 1)
            pool.affine_select(out=ident[:], in_=ident[:], compare_op=ALU.not_equal, fill=1.0, base=0,
                               pattern=[[-1, 128]], channel_multiplier=1).then_inc(s_ident, 1)
            pool.wait_ge(s_whi, 1)
            pool.tensor_tensor(qk_lo[:], attn_w_s[:, 0:2, :], qk_hi[:].bitcast(F32), ALU.subtract).then_inc(s_wlo, 1)
            for u in range(2):
                pool.memset(va[u][:], 0.0).then_inc(s_va0, 1)
                pool.wait_ge(s_va0, 2 * u + 1)
                pool.memset(va[u][:, :, :, DH:DH + 1], 1.0).then_inc(s_va0, 1)
            pool.wait_ge(s_whi, 2)
            pool.tensor_tensor(ffn_lo[:], ffn_in_s[:], ffn_hi[:].bitcast(F32), ALU.subtract).then_inc(s_wlo, 1)
            pool.wait_ge(s_mhalf, 2)
            run_steps(pool, step)


def kernel(x, cond_256, L0_cond_Wq, L0_cond_Wk, L0_cond_Wv, L0_cond_Wo, L0_cond_g1w, L0_cond_g1b, L0_cond_b1w,
           L0_cond_b1b, L0_cond_g2w, L0_cond_g2b, L0_cond_b2w, L0_cond_b2b, L0_cond_gate_w, L0_cond_hid_w,
           L0_cond_out_w):
    import numpy as np
    import concourse.bacc as bacc
    from concourse.bass_utils import run_bass_kernel_spmd

    heads, dim = 16, 128
    x, cond = np.asarray(x), np.asarray(cond_256)
    wq, wk, wv, wo = (np.asarray(w) for w in (L0_cond_Wq, L0_cond_Wk, L0_cond_Wv, L0_cond_Wo))

    def dim_head(w):
        return w.reshape(heads, dim // heads, dim).transpose(1, 0, 2).reshape(dim, dim)

    hid = np.asarray(L0_cond_gate_w).shape[0]
    arrays = {
        "x": x.transpose(1, 0, 2),
        "cond": cond.T,
        "mod_w": np.stack([np.asarray(w).T for w in (L0_cond_g1w, L0_cond_b1w, L0_cond_g2w, L0_cond_b2w)], axis=1),
        "mod_b": np.stack([np.asarray(b) for b in (L0_cond_g1b, L0_cond_b1b, L0_cond_g2b, L0_cond_b2b)], axis=1),
        "attn_w": np.stack([dim_head(wq).T, dim_head(wk).T, wv.T, wo.T], axis=1),
        "ffn_in_w": np.stack([np.asarray(L0_cond_gate_w).T, np.asarray(L0_cond_hid_w).T], axis=1),
        "ffn_out_w": np.asarray(L0_cond_out_w).T.reshape(hid // 128, 128, dim).transpose(1, 0, 2),
    }
    arrays = {f"in_{n}": np.ascontiguousarray(a) for n, a in arrays.items()}
    nc = bacc.Bacc("TRN2", target_bir_lowering=False, num_devices=1)
    aps = [nc.dram_tensor(n, a.shape, mybir.dt.from_np(a.dtype), kind="ExternalInput").ap() for n, a in arrays.items()]
    batch, length, _ = x.shape
    out = nc.dram_tensor("out_y", (length, batch, dim), F32, kind="ExternalOutput").ap()
    bass_cond_transformer_block(nc, *aps, out)
    r = run_bass_kernel_spmd(nc, [arrays], core_ids=[0])
    return np.ascontiguousarray(r.results[0]["out_y"].transpose(1, 0, 2))
```

```python
from contextlib import ExitStack

import concourse.bass as bass
from concourse import mybir

ALU = mybir.AluOpType
ACT = mybir.ActivationFunctionType
AX = mybir.AxisListType
F32 = mybir.dt.float32
F32R = mybir.dt.float32r
BF16 = mybir.dt.bfloat16

EPS = 1e-6


def bass_cond_transformer_block(
    nc: bass.Bass,
    x: bass.AP,
    cond: bass.AP,
    mod_w: bass.AP,
    mod_b: bass.AP,
    attn_w: bass.AP,
    ffn_in_w: bass.AP,
    ffn_out_w: bass.AP,
    out: bass.AP,
):
    L, B, D = x.shape
    DT = cond.shape[0]
    H = 16
    DH = D // H
    HC = ffn_out_w.shape[1]
    NB = 4
    G = B // NB
    W = NB * L
    HQ = 4
    CH = H // HQ
    NK = NB * CH
    NP = 4
    VW = 32
    PARTS = 3
    Q_PART = [0, 0, 0, 1, 1, 2]
    K_PART = [0, 1, 2, 0, 1, 0]
    ROWS = DH * len(Q_PART)
    RAW_ROWS = 96
    SHIFT = RAW_ROWS
    STK = 16 * 2 * len(Q_PART)
    SCALE = float(DH) ** -0.5
    assert D == 128 and L == 128 and W == 512 and B % (2 * NB) == 0 and H * DH == D and HC == 4

    PV_LAG = 2
    RAW_LAG = 3
    OT, TR4, NORM, TRO, OTC, WO, X1 = 5, 7, 8, 9, 10, 10, 11
    XT2, XN2, HI2 = 14, 14, 15
    MS_SLOT, XT1, XN1 = -2, 0, 0
    HI1 = 5
    V_SLOT = -2
    Q_SLOT, QHI, QREST, QMID, QLO = 15, 16, 19, 20, 20
    K_SLOT, KHI, KREST, KMID, KLO = 16, 18, 19, 20, 20
    CT_SLOT, SHIFT_SLOT = 19, 19
    FFN_SLOT = -2
    FFN_LATE = 5
    FIRST_SLOT, LAST_SLOT = -2, 20
    SLOTS = LAST_SLOT - FIRST_SLOT + 1
    HALF = NB // 2

    ctx = ExitStack()
    with ctx:
        def sb(name, shape, dt=F32):
            return ctx.enter_context(nc.sbuf_tensor(name, shape, dt))

        def bank(name):
            return ctx.enter_context(nc.psum_tensor(name, [128, 512], F32))

        def sem(name):
            return ctx.enter_context(nc.semaphore(name))

        cond_s = sb("cond_s", [DT, B])
        mod_w_s = sb("mod_w_s", [DT, 4, D])
        mod_b_s = sb("mod_b_s", [D, 4])
        attn_w_s = sb("attn_w_s", [D, 4, D])
        ffn_in_s = sb("ffn_in_s", [D, 2, HC * 128])
        ffn_out_s = sb("ffn_out_s", [128, HC, D])
        qk_hi = sb("qk_hi", [D, 2, D], F32R)
        qk_lo = sb("qk_lo", [D, 2, D], F32R)
        ffn_hi = sb("ffn_hi", [D, 2, HC * 128], F32R)
        ffn_lo = sb("ffn_lo", [D, 2, HC * 128], F32R)
        mod = sb("mod", [D, 4, B])
        ident = sb("ident", [128, 128])
        mhalf = sb("mhalf", [128, NB])
        ones = sb("ones", [H * NB, L], BF16)
        x_s = sb("x_s", [L, B * D])
        sqx = sb("sqx", [L, NB, D])
        sq1 = sb("sq1", [L, NB])
        ms1 = sb("ms1", [L, NB])
        inv1 = sb("inv1", [L, NB])
        xs1 = sb("xs1", [L, NB, D])
        xn1 = sb("xn1", [D, NB, L])
        xn1_hi = sb("xn1_hi", [D, W], F32R)
        xn1_lo = sb("xn1_lo", [D, W], F32R)
        qp = sb("qp", [D, PARTS, W], BF16)
        kp = sb("kp", [D, PARTS, W], BF16)
        q_rest = sb("q_rest", [D, W])
        k_rest = sb("k_rest", [D, W])
        qs = [sb(f"qs{u}", [128, H, W], BF16) for u in range(2)]
        ks = [sb(f"ks{u}", [128, H, W], BF16) for u in range(2)]
        va = [sb(f"va{u}", [L, NB, H, VW]) for u in range(2)]
        nmax = sb("nmax", [L, 128])
        shift = sb("shift", [H * NB, 2, L], BF16)
        p_s = sb("p_s", [L, NP, HQ * L])
        ot_s = sb("ot_s", [128, 2, CH * L])
        rden = sb("rden", [L, H])
        o_s = sb("o_s", [L, D])
        oT_s = sb("oT_s", [D, L])
        x1 = sb("x1", [L, NB, D])
        sqx1 = sb("sqx1", [L, NB, D])
        ms2 = sb("ms2", [L, NB])
        inv2 = sb("inv2", [L, NB])
        xs2 = sb("xs2", [L, NB, D])
        xn2 = sb("xn2", [D, NB, L])
        xn2_hi = sb("xn2_hi", [D, 2, NB, L], F32R)
        xn2_lo = sb("xn2_lo", [D, 2, NB, L], F32R)
        th = sb("th", [128, 2, W])
        gated = sb("gated", [128, W])
        hT = sb("hT", [128, 2, W])
        resid = sb("resid", [L, 2, NB, D])

        score = [bank("score0"), bank("score1")]
        gate_up = [bank("gate"), bank("up")]
        pv = [bank("pv0"), bank("pv1")]
        ffn_y = pv[1]
        tok = bank("tok")
        small = bank("small")

        def ffn_banks(ch):
            return score if ch == 1 else gate_up

        s_x = [sem("s_xin0"), sem("s_xin1")]
        s_xrest = sem("s_xrest")
        s_modw, s_modb, s_attnw, s_ffnin, s_ffnout = sem("s_modw"), sem("s_modb"), sem("s_attnw"), sem("s_ffnin"), sem("s_ffnout")
        s_stack = [sem("s_stack0"), sem("s_stack1")]
        s_shiftrow = [sem("s_shiftrow0"), sem("s_shiftrow1")]
        s_out = sem("s_out")
        s_ident0, s_ident, s_mhalf, s_nmax0, s_ones, s_table = (sem("s_ident0"), sem("s_ident"), sem("s_mhalf"),
                                                                sem("s_nmax0"), sem("s_ones"), sem("s_table"))
        s_va0 = [sem("s_va00"), sem("s_va01")]
        s_onerows = sem("s_onerows")
        s_zeroq, s_zerok = [sem("s_zeroq0"), sem("s_zeroq1")], [sem("s_zerok0"), sem("s_zerok1")]
        s_modp, s_mod, s_whi, s_wlo = sem("s_modp"), sem("s_mod"), sem("s_whi"), sem("s_wlo")
        s_sq1 = sem("s_sq1")
        s_ms1, s_inv1, s_xs1, s_xt1, s_xn1, s_hi1, s_lo1 = (sem("s_ms1"), sem("s_inv1"), sem("s_xs1"), sem("s_xt1"),
                                                            sem("s_xn1"), sem("s_hi1"), sem("s_lo1"))
        s_v, s_va = sem("s_v"), sem("s_va")
        s_q, s_qhi, s_qrest, s_qmid, s_qlo = sem("s_q"), sem("s_qhi"), sem("s_qrest"), sem("s_qmid"), sem("s_qlo")
        s_k, s_khi, s_krest, s_kmid, s_klo = sem("s_k"), sem("s_khi"), sem("s_krest"), sem("s_kmid"), sem("s_klo")
        s_raw, s_max, s_maxT, s_shi, s_slo = sem("s_raw"), sem("s_max"), sem("s_maxT"), sem("s_shi"), sem("s_slo")
        s_score, s_exp, s_pv, s_ot, s_tr4, s_rden = (sem("s_score"), sem("s_exp"), sem("s_pv"), sem("s_ot"),
                                                     sem("s_tr4"), sem("s_rden"))
        s_o, s_oTp, s_oT, s_wo, s_x1 = sem("s_o"), sem("s_oTp"), sem("s_oT"), sem("s_wo"), sem("s_x1")
        s_ms2, s_inv2, s_xs2, s_xt2, s_xn2, s_hi2, s_lo2 = (sem("s_ms2"), sem("s_inv2"), sem("s_xs2"), sem("s_xt2"),
                                                            sem("s_xn2"), sem("s_hi2"), sem("s_lo2"))
        s_gate, s_up, s_tanh, s_gated, s_h, s_y, s_resid, s_fin = (
            sem("s_gate"), sem("s_up"), sem("s_tanh"), sem("s_gated"), sem("s_h"), sem("s_y"), sem("s_resid"),
            sem("s_fin"))

        def num(g):
            return g[0] * 2 + g[1]

        def plus(g, n):
            return (g[0] + (g[1] + n) // 2, (g[1] + n) % 2)

        def first(g):
            return isinstance(g[0], int) and num(g) == 0

        def cols(g):
            return bass.ds(num(g) * W, W)

        def places(w):
            if isinstance(w[0], int):
                return {0: (HALF, NB), G: (0, HALF)}.get(num(w), (0, NB))
            return 0, NB

        def window_cols(w):
            p0, p1 = places(w)
            return bass.ds(num(w) * W + (p0 - HALF) * D, (p1 - p0) * D)

        def in_window(g, b):
            return (g[1] + (b >= HALF)) % 2, (b + HALF) % NB

        def run_steps(eng, step, rest=None):
            last = (G // 2 - 1, 1)
            step(None, None, None, (0, 0))
            step(None, None, None, (0, 1), v=(0, 0))
            if rest is not None:
                rest()
            step(None, None, (0, 0), None, v=(0, 1))
            step(None, (0, 0), (0, 1), (1, 0))
            step((0, 0), (0, 1), (1, 0), (1, 1), v=(1, 0))
            with eng.Fori(1, G // 2 - 1) as i:
                for u in range(2):
                    step(plus((i, u), -1), (i, u), plus((i, u), 1), plus((i, u), 2), v=plus((i, u), 1))
            step(plus(last, -2), plus(last, -1), last, None, v=last)
            step(plus(last, -1), last, None, None)
            step(last, None, None, None, late=(G // 2, 0))

        def in_slot(p, c, s):
            return ([] if p is None else [(p, s + SLOTS)]) + ([] if c is None else [(c, s)])

        def windows(p, c, late):
            return ([(p, FFN_SLOT)] if p is not None else []) + (
                [(late, FFN_LATE)] if late is not None else [])

        block = ctx.enter_context(nc.Block())

        @block.sync
        def _(sp):
            def ahead(value):
                return value if isinstance(value, int) else sp.compute_val(value)

            def stack_rows(g, n, dst, parts, part_of, part, ready):
                sp.wait_ge(ready, n)
                for r in range(len(part_of)):
                    if part_of[r] == part:
                        sp.dma_start(dst[g[1]][DH * r:DH * r + DH, :, :].rearrange("d h w -> d (h w)"),
                                     parts[:, part, :]).then_inc(s_stack[g[1]], 16)

            def step(p, c, b, a, v=None, late=None):
                stores = []
                for w, _ in windows(p, c, late):
                    p0, p1 = places(w)
                    stores.append((ahead(num(w) * W + (p0 - HALF) * D), (p1 - p0) * D, ahead(num(w) + 1)))
                if c is not None:
                    scores_before, scores_done = ahead(NK * num(c)), ahead(NK * (num(c) + 1))
                if b is not None:
                    b_done = ahead(num(b) + 1)
                if a is not None:
                    a_done = ahead(num(a) + 1)
                for at, width, done in stores:
                    sp.wait_ge(s_fin, done)
                    sp.dma_start(out.rearrange("l b d -> l (b d)")[:, bass.ds(at, width)],
                                 x_s[:, bass.ds(at, width)]).then_inc(s_out, 16)
                if b is not None:
                    if c is not None:
                        sp.wait_ge(s_score, scores_before)
                    sp.wait_ge(s_shi, b_done)
                    sp.dma_start(qs[b[1]][SHIFT:SHIFT + 1, :, :].rearrange("d h w -> d (h w)"),
                                 shift[:, 0, :]).then_inc(s_shiftrow[b[1]], 16)
                    sp.wait_ge(s_slo, b_done)
                    sp.dma_start(qs[b[1]][SHIFT + 1:SHIFT + 2, :, :].rearrange("d h w -> d (h w)"),
                                 shift[:, 1, :]).then_inc(s_shiftrow[b[1]], 16)
                if a is not None:
                    if c is not None:
                        sp.wait_ge(s_score, scores_done)
                    else:
                        sp.wait_ge(s_zeroq[a[1]], 1)
                        sp.wait_ge(s_zerok[a[1]], 1)
                        sp.wait_ge(s_ones, 1)
                        for row in (SHIFT, SHIFT + 1):
                            sp.dma_start(ks[a[1]][row:row + 1, :, :].rearrange("d h w -> d (h w)"),
                                         ones[:]).then_inc(s_onerows, 16)
                    stack_rows(a, a_done, qs, qp, Q_PART, 0, s_qhi)
                    stack_rows(a, a_done, qs, qp, Q_PART, 1, s_qmid)
                    stack_rows(a, a_done, ks, kp, K_PART, 0, s_khi)
                    stack_rows(a, a_done, ks, kp, K_PART, 1, s_kmid)
                    stack_rows(a, a_done, qs, qp, Q_PART, 2, s_qlo)
                    stack_rows(a, a_done, ks, kp, K_PART, 2, s_klo)

            x_cols = x.rearrange("l b d -> l (b d)")
            sp.dma_start(x_s[:, 0:W], x_cols[:, 0:W]).then_inc(s_x[0], 16)
            sp.dma_start(mod_b_s[:], mod_b).then_inc(s_modb, 16)
            sp.dma_start(attn_w_s[:], attn_w).then_inc(s_attnw, 16)
            sp.dma_start(x_s[:, W:2 * W], x_cols[:, W:2 * W]).then_inc(s_x[1], 16)
            sp.dma_start(ffn_in_s[:], ffn_in_w).then_inc(s_ffnin, 16)
            sp.dma_start(ffn_out_s[:], ffn_out_w).then_inc(s_ffnout, 16)
            sp.dma_start(x_s[:, 2 * W:], x_cols[:, 2 * W:]).then_inc(s_xrest, 16)

            run_steps(sp, step)
            sp.wait_ge(s_out, 16 * (G + 1))

        @block.tensor
        def _(pe):
            def split_product(dst, w_hi, w_lo, v_hi, v_lo):
                pe.matmul(dst, w_hi, v_hi, start=True, stop=False)
                pe.matmul(dst, w_hi, v_lo, start=False, stop=False)
                return pe.matmul(dst, w_lo, v_hi, start=False, stop=True)

            def a_transpose(g, c, b):
                pe.wait_ge(s_xs1, num(g) + 1)
                pe.wait_ge(s_xn1, NB * num(g) + b)
                if c is not None and b == 0:
                    pe.wait_ge(s_x1, NB * num(c))
                if c is not None and b == 3:
                    pe.wait_ge(s_x1, NB * num(c) + 1)
                pe.transpose(small[:, 0:L], xs1[:, b, :], ident[:]).then_inc(s_xt1, 1)

            def a_values(g, c):
                pe.wait_ge(s_xn1, NB * (num(g) + 1))
                pe.wait_ge(s_va, num(g))
                if c is not None:
                    pe.wait_ge(s_slo, num(g))
                for b in range(NB):
                    mm = pe.matmul(pv[0][:, b * L:(b + 1) * L], xn1[:, b, :], attn_w_s[:, 2, :], start=True, stop=True)
                mm.then_inc(s_v, 1)

            def a_query(g, c):
                if c is not None:
                    pe.wait_ge(s_exp, NK * (num(c) + 1) - 1)
                else:
                    pe.wait_ge(s_qrest, num(g))
                pe.wait_ge(s_lo1, 2 * (num(g) + 1))
                if first(g):
                    pe.wait_ge(s_wlo, 1)
                split_product(score[0][:], qk_hi[:, 0, :], qk_lo[:, 0, :], xn1_hi[:], xn1_lo[:]).then_inc(s_q, 1)

            def a_key(g, c):
                if c is not None:
                    pe.wait_ge(s_exp, NK * (num(c) + 1))
                else:
                    pe.wait_ge(s_krest, num(g))
                split_product(score[1][:], qk_hi[:, 1, :], qk_lo[:, 1, :], xn1_hi[:], xn1_lo[:]).then_inc(s_k, 1)

            def b_raw(g, p, k):
                b, ch = k // CH, k % CH
                if k == 0:
                    pe.wait_ge(s_stack[g[1]], STK * (g[0] + 1))
                    if p is not None:
                        pe.wait_ge(s_h, HC * (num(p) + 1))
                if k >= 2:
                    pe.wait_ge(s_max, NK * num(g) + k - 1)
                for j in range(HQ):
                    h = ch * HQ + j
                    mm = pe.matmul(gate_up[k % 2][:, j * L:(j + 1) * L], qs[g[1]][0:RAW_ROWS, h, b * L:(b + 1) * L],
                                   ks[g[1]][0:RAW_ROWS, h, b * L:(b + 1) * L], start=True, stop=True)
                mm.then_inc(s_raw, 1)

            def b_maxT(g, c):
                pe.wait_ge(s_max, NK * (num(g) + 1))
                if c is None:
                    pe.wait_ge(s_nmax0, 1)
                    pe.wait_ge(s_va, 2)
                else:
                    pe.wait_ge(s_ot, NB * num(c) + 3)
                pe.transpose(pv[0][:, 0:L], nmax[:], ident[:]).then_inc(s_maxT, 1)

            def c_scores(g, p, k):
                b, ch = k // CH, k % CH
                if k == 0:
                    pe.wait_ge(s_shiftrow[g[1]], 32 * (g[0] + 1))
                    pe.wait_ge(s_exp, NK * num(g))
                    ready = min(num(g) + 2, G) if isinstance(g[0], int) else num(g) + 2
                    pe.wait_ge(s_qrest, ready)
                    pe.wait_ge(s_krest, ready)
                    if first(g):
                        pe.wait_ge(s_onerows, 64)
                    if p is not None:
                        pe.wait_ge(s_h, HC * num(p) + 2)
                if k >= 2:
                    pe.wait_ge(s_exp, NK * num(g) + k - 1)
                for j in range(HQ):
                    h = ch * HQ + j
                    mm = pe.matmul(score[k % 2][:, j * L:(j + 1) * L], ks[g[1]][:, h, b * L:(b + 1) * L],
                                   qs[g[1]][:, h, b * L:(b + 1) * L], start=True, stop=True)
                mm.then_inc(s_score, 1)

            def c_pv(g, p, k):
                b, ch = k // CH, k % CH
                if k == 0:
                    pe.wait_ge(s_va, min(num(g) + 2, G) if isinstance(g[0], int) else num(g) + 2)
                    pe.wait_ge(s_slo, num(g) + 1)
                    pe.wait_ge(s_ot, NB * num(g))
                if k == CH and p is not None:
                    pe.wait_ge(s_fin, num(p) + 1)
                if ch == 0 and b >= 2:
                    pe.wait_ge(s_ot, NB * num(g) + b - 1)
                pe.wait_ge(s_exp, NK * num(g) + k + 1)
                for j in range(HQ):
                    h = ch * HQ + j
                    mm = pe.matmul(pv[b % 2][VW * j:VW * j + VW, ch * L:(ch + 1) * L], va[g[1]][:, b, h, :],
                                   p_s[:, k % NP, j * L:(j + 1) * L], start=True, stop=True)
                mm.then_inc(s_pv, 1)

            def c_tr4(g, b):
                pe.wait_ge(s_ot, NB * num(g) + b + 1)
                pe.wait_ge(s_o, NB * num(g) + b)
                pe.wait_ge(s_xn2, NB * num(g) + max(b - 1, 0))
                for ch in range(CH):
                    mm = pe.transpose(tok[:, ch * 128:(ch + 1) * 128], ot_s[:, b % 2, ch * L:(ch + 1) * L], ident[:])
                mm.then_inc(s_tr4, 1)

            def c_tro(g, b, a):
                pe.wait_ge(s_o, NB * num(g) + b + 1)
                pe.wait_ge(s_x1, NB * num(g) + b)
                if a is not None and b < 2:
                    pe.wait_ge(s_xn1, NB * num(a) + b + 3)
                pe.transpose(small[:, 0:L], o_s[:], ident[:]).then_inc(s_oTp, 1)

            def c_wo(g, b):
                pe.wait_ge(s_oT, NB * num(g) + b + 1)
                pe.matmul(small[:, L:2 * L], oT_s[:], attn_w_s[:, 3, :], start=True, stop=True).then_inc(s_wo, 1)

            def d_xt2(g, b):
                pe.wait_ge(s_xs2, NB * num(g) + b + 1)
                pe.wait_ge(s_o, NB * num(g) + min(b + 2, NB))
                pe.wait_ge(s_xn2, NB * num(g) + b)
                pe.transpose(tok[:, 0:L], xs2[:, b, :], ident[:]).then_inc(s_xt2, 1)

            def d_gate_up(w, c, ch):
                if first(w) and ch == 0:
                    pe.wait_ge(s_wlo, 2)
                if ch == 0:
                    if isinstance(w[0], int):
                        pe.wait_ge(s_lo2, min(NB * num(w) + HALF, NB * G))
                        b_done = min(num(w) + 2, G)
                    else:
                        pe.wait_ge(s_lo2, NB * num(w) + HALF)
                        b_done = num(w) + 2
                    pe.wait_ge(s_max, NK * b_done)
                    pe.wait_ge(s_h, HC * num(w))
                elif ch == 1:
                    ready = min(num(w) + 3, G) if isinstance(w[0], int) else num(w) + 3
                    pe.wait_ge(s_qrest, ready)
                    pe.wait_ge(s_krest, ready)
                    pe.wait_ge(s_exp, min(NK * (num(w) + 1), NK * G) if isinstance(w[0], int) else NK * (num(w) + 1))
                    pe.wait_ge(s_h, HC * num(w))
                else:
                    before = {2: 0, 3: 2}[ch]
                    pe.wait_ge(s_gated, HC * num(w) + before + 1)
                p0, p1 = places(w)
                cs, ns = slice(ch * 128, ch * 128 + 128), slice(p0 * L, p1 * L)
                hi, lo = (x[:, w[1], p0:p1, :].rearrange("d b l -> d (b l)") for x in (xn2_hi, xn2_lo))
                gate, up = ffn_banks(ch)
                split_product(gate[:, ns], ffn_hi[:, 0, cs], ffn_lo[:, 0, cs], hi, lo).then_inc(s_gate, 1)
                if ch > 1:
                    pe.wait_ge(s_h, HC * num(w) + before + 1)
                split_product(up[:, ns], ffn_hi[:, 1, cs], ffn_lo[:, 1, cs], hi, lo).then_inc(s_up, 1)

            def d_out(w, ch):
                if first(w) and ch == 0:
                    pe.wait_ge(s_ffnout, 16)
                if ch == 0:
                    pe.wait_ge(s_ot, min(NB * (num(w) + 1), NB * G) if isinstance(w[0], int) else NB * (num(w) + 1))
                    pe.wait_ge(s_fin, num(w))
                pe.wait_ge(s_h, HC * num(w) + ch + 1)
                p0, p1 = places(w)
                for p in range(p0, p1):
                    mm = pe.matmul(ffn_y[:, p * D:(p + 1) * D], hT[:, ch % 2, p * L:(p + 1) * L], ffn_out_s[:, ch, :],
                                   start=(ch == 0 and p == p0), stop=(ch == HC - 1), skip_group_check=True)
                mm.then_inc(s_y, 1)

            def step(p, c, b, a, v=None, late=None):
                for s in range(FIRST_SLOT, LAST_SLOT + 1):
                    for w, first in windows(p, c, late):
                        if 0 <= s - first < HC:
                            d_gate_up(w, c, s - first)
                    if a is not None and s in range(XT1, XT1 + 4 * NB, 4):
                        a_transpose(a, c, (s - XT1) // 4)
                    if c is not None and 0 <= s < NK:
                        c_scores(c, p, s)
                    if c is not None and 0 <= s - PV_LAG < NK:
                        c_pv(c, p, s - PV_LAG)
                    for w, first in windows(p, c, late):
                        if 0 <= s - first - 1 < HC:
                            d_out(w, s - first - 1)
                    if b is not None and 0 <= s - RAW_LAG < NK:
                        b_raw(b, p, s - RAW_LAG)
                    if v is not None and s == V_SLOT:
                        a_values(v, c)
                    for g, at in in_slot(p, c, s):
                        for n in range(NB):
                            if at == 4 * n + TR4:
                                c_tr4(g, n)
                            if at == 4 * n + TRO:
                                c_tro(g, n, a)
                            if at == 4 * n + WO:
                                c_wo(g, n)
                            if at == 4 * n + XT2:
                                d_xt2(g, n)
                    if b is not None and s == CT_SLOT:
                        b_maxT(b, c)
                    if a is not None and s == Q_SLOT:
                        a_query(a, c)
                    if a is not None and s == K_SLOT:
                        a_key(a, c)

            pe.wait_ge(s_modw, 32)
            for i in range(4):
                mm = pe.matmul(small[:, i * B:(i + 1) * B], mod_w_s[:, i, :], cond_s[:], start=True, stop=True)
            mm.then_inc(s_modp, 1)
            pe.wait_ge(s_mod, 4)
            pe.wait_ge(s_ident, 1)
            run_steps(pe, step)

        @block.scalar
        def _(act):
            def a_norm(g, b):
                act.wait_ge(s_xt1, NB * num(g) + b + 1)
                if b == 0:
                    act.wait_ge(s_v, num(g))
                    act.wait_ge(s_lo1, 2 * num(g))
                act.activation(xn1[:, b, :], small[:, 0:L], ACT.Identity,
                               scale=mod[:, 0, bass.ds(num(g) * NB + b, 1)],
                               bias=mod[:, 1, bass.ds(num(g) * NB + b, 1)]).then_inc(s_xn1, 1)

            def a_values(g, c):
                act.wait_ge(s_v, num(g) + 1)
                if isinstance(g[0], int) and num(g) < 2:
                    act.wait_ge(s_va0[num(g)], 2)
                else:
                    act.wait_ge(s_pv, NK * (num(g) - 1))
                act.activation(va[g[1]][:, :, :, 0:DH].rearrange("l b h d -> l (b h) d"),
                               pv[0][:].rearrange("l (n d) -> l n d", d=DH), ACT.Copy).then_inc(s_va, 1)

            def a_high(g, ready, src, dst, done):
                act.wait_ge(ready, num(g) + 1)
                before = plus(g, -1)
                if not (isinstance(g[0], int) and num(g) == 0):
                    act.wait_ge(s_stack[before[1]], STK * (before[0] + 1))
                act.activation(dst[:, 0, :], src[:], ACT.Copy).then_inc(done, 1)

            def a_middle(g, ready, rest, dst, done):
                act.wait_ge(ready, num(g) + 1)
                act.activation(dst[:, 1, :], rest[:], ACT.Copy).then_inc(done, 1)

            def c_exp(g, k):
                act.wait_ge(s_score, NK * num(g) + k + 1)
                if k == 0:
                    act.wait_ge(s_pv, NK * num(g))
                if k >= NP:
                    act.wait_ge(s_pv, NK * num(g) + k - NP + 1)
                act.activation(p_s[:, k % NP, :], score[k % 2][:], ACT.Exp, scale=SCALE).then_inc(s_exp, 1)

            def c_ot(g, b):
                act.wait_ge(s_pv, NK * num(g) + CH * (b + 1))
                if b >= 2:
                    act.wait_ge(s_tr4, NB * num(g) + b - 1)
                else:
                    act.wait_ge(s_tr4, NB * num(g))
                act.activation(ot_s[:, b % 2, :], pv[b % 2][:], ACT.Copy).then_inc(s_ot, 1)

            def c_oT(g, b):
                act.wait_ge(s_oTp, NB * num(g) + b + 1)
                act.wait_ge(s_wo, NB * num(g) + b)
                act.activation(oT_s[:], small[:, 0:L], ACT.Copy).then_inc(s_oT, 1)

            def d_norm(g, b):
                act.wait_ge(s_xt2, NB * num(g) + b + 1)
                act.wait_ge(s_lo2, NB * num(g))
                act.activation(xn2[:, b, :], tok[:, 0:L], ACT.Identity,
                               scale=mod[:, 2, bass.ds(num(g) * NB + b, 1)],
                               bias=mod[:, 3, bass.ds(num(g) * NB + b, 1)]).then_inc(s_xn2, 1)

            def d_tanh(w, ch):
                act.wait_ge(s_gate, HC * num(w) + ch + 1)
                if ch < 2:
                    act.wait_ge(s_gated, HC * num(w))
                else:
                    act.wait_ge(s_gated, HC * num(w) + ch - 1)
                ns = slice(places(w)[0] * L, places(w)[1] * L)
                act.activation(th[:, ch % 2, ns], ffn_banks(ch)[0][:, ns], ACT.Tanh, scale=0.5).then_inc(s_tanh, 1)

            def step(p, c, b, a, v=None, late=None):
                for s in range(FIRST_SLOT, LAST_SLOT + 1):
                    for w, first in windows(p, c, late):
                        if 0 <= s - first < HC:
                            d_tanh(w, s - first)
                    for g, at in in_slot(p, c, s):
                        for n in range(NB):
                            if at == 4 * n + OTC:
                                c_oT(g, n)
                    if a is not None and s in range(XN1, XN1 + 4 * NB, 4):
                        a_norm(a, (s - XN1) // 4)
                    if c is not None and 0 <= s < NK:
                        c_exp(c, s)
                    for g, at in in_slot(p, c, s):
                        for n in range(NB):
                            if at == 4 * n + OT:
                                c_ot(g, n)
                            if at == 4 * n + XN2:
                                d_norm(g, n)
                    if v is not None and s == V_SLOT:
                        a_values(v, c)
                    if a is not None and s == QHI:
                        a_high(a, s_q, score[0], qp, s_qhi)
                    if a is not None and s == QMID:
                        a_middle(a, s_qrest, q_rest, qp, s_qmid)
                    if a is not None and s == KHI:
                        a_high(a, s_k, score[1], kp, s_khi)
                    if a is not None and s == KMID:
                        a_middle(a, s_krest, k_rest, kp, s_kmid)

            act.dma_start(mod_w_s[:], mod_w).then_inc(s_modw, 16)
            act.dma_start(cond_s[:], cond).then_inc(s_modw, 16)
            act.wait_ge(s_mhalf, 1)
            act.activation(th[:, 0, 0:NB], mhalf[:], ACT.Exp).then_inc(s_table, 1)
            act.wait_ge(s_modp, 1)
            act.wait_ge(s_modb, 16)
            for i in range(4):
                act.activation(mod[:, i, :], small[:, i * B:(i + 1) * B], ACT.Identity,
                               bias=mod_b_s[:, i:i + 1]).then_inc(s_mod, 1)
            act.wait_ge(s_mod, 4)
            run_steps(act, step)

        @block.vector
        def _(dve):
            def a_mean(g, c):
                if c is None:
                    dve.wait_ge(s_x[g[1]], 16)
                else:
                    dve.wait_ge(s_xrest, 16)
                dve.wait_ge(s_ms1, num(g))
                for b in range(NB):
                    xb = x_s[:, bass.ds(num(g) * W + b * D, D)]
                    dve.scalar_tensor_tensor(out=sqx[:, b, :], in0=xb, scalar=1.0 / D, in1=xb, op0=ALU.mult, op1=ALU.mult,
                                             accum_out=sq1[:, b:b + 1]).then_inc(s_sq1, 1)
                dve.wait_ge(s_sq1, NB * (num(g) + 1))
                dve.tensor_scalar(ms1[:], sq1[:], EPS, None, ALU.add).then_inc(s_ms1, 1)

            def a_hi(g, n):
                dve.wait_ge(s_xn1, NB * num(g) + 2 * n + 2)
                if n == 0:
                    dve.wait_ge(s_k, num(g))
                    dve.wait_ge(s_lo1, 2 * num(g))
                dve.tensor_copy(xn1_hi[:, 2 * n * L:2 * (n + 1) * L],
                                xn1[:, 2 * n:2 * n + 2, :].rearrange("d b l -> d (b l)")).then_inc(s_hi1, 1)

            def a_rest(g, src, parts, rest, high, lowest, done):
                dve.wait_ge(high, num(g) + 1)
                dve.wait_ge(lowest, num(g))
                dve.tensor_tensor(rest[:], src[:], parts[:, 0, :], ALU.subtract).then_inc(done, 1)

            def b_max(g, k):
                b, ch = k // CH, k % CH
                dve.wait_ge(s_raw, NK * num(g) + k + 1)
                if k == 0 and first(g):
                    dve.wait_ge(s_nmax0, 1)
                if k == 0:
                    dve.wait_ge(s_maxT, num(g))
                heads = nmax[:, ch * HQ * NB:(ch + 1) * HQ * NB].rearrange("l (j b) -> l j b", b=NB)
                dve.tensor_reduce(heads[:, :, b], gate_up[k % 2][:].rearrange("l (j m) -> l j m", j=HQ),
                                  AX.X, ALU.max, negate=True).then_inc(s_max, 1)

            def b_shift(g):
                dve.wait_ge(s_maxT, num(g) + 1)
                before = plus(g, -1)
                if not (isinstance(g[0], int) and num(g) == 0):
                    dve.wait_ge(s_shiftrow[before[1]], 32 * (before[0] + 1))
                dve.tensor_copy(shift[:, 0, :], pv[0][0:H * NB, 0:L]).then_inc(s_shi, 1)
                dve.wait_ge(s_shi, num(g) + 1)
                dve.tensor_tensor(shift[:, 1, :], pv[0][0:H * NB, 0:L], shift[:, 0, :],
                                  ALU.subtract).then_inc(s_slo, 1)

            def c_norm(g, b):
                dve.wait_ge(s_tr4, NB * num(g) + b + 1)
                heads = tok[:].rearrange("l (h v) -> l h v", v=VW)
                dve.reciprocal(rden[:], heads[:, :, DH]).then_inc(s_rden, 1)
                dve.wait_ge(s_rden, NB * num(g) + b + 1)
                dve.wait_ge(s_oTp, NB * num(g) + b)
                dve.tensor_tensor(o_s[:].rearrange("l (h d) -> l h d", h=H), heads[:, :, 0:DH],
                                  rden[:].unsqueeze(2).to_broadcast([L, H, DH]), ALU.mult).then_inc(s_o, 1)

            def c_x1(g, b):
                dve.wait_ge(s_wo, NB * num(g) + b + 1)
                if b == 0:
                    dve.wait_ge(s_resid, 2 * num(g))
                dve.tensor_tensor(x1[:, b, :], small[:, L:2 * L], x_s[:, bass.ds(num(g) * W + b * D, D)],
                                  ALU.add).then_inc(s_x1, 1)
                dve.wait_ge(s_x1, NB * num(g) + b + 1)
                dve.wait_ge(s_ms2, NB * num(g))
                dve.tensor_tensor_reduce(sqx1[:, b, :], x1[:, b, :], x1[:, b, :], 1.0 / D, EPS, ALU.mult, ALU.add,
                                         ms2[:, b:b + 1]).then_inc(s_ms2, 1)

            def d_hi(g, b):
                dve.wait_ge(s_xn2, NB * num(g) + b + 1)
                if b == HALF:
                    dve.wait_ge(s_up, HC * num(g))
                    dve.wait_ge(s_lo2, NB * num(g) + HALF)
                u, p = in_window(g, b)
                dve.tensor_copy(xn2_hi[:, u, p, :], xn2[:, b, :]).then_inc(s_hi2, 1)

            def d_hidden(w, ch):
                ns = slice(places(w)[0] * L, places(w)[1] * L)
                dve.wait_ge(s_tanh, HC * num(w) + ch + 1)
                dve.wait_ge(s_h, HC * num(w) + ch)
                dve.scalar_tensor_tensor(out=gated[:, ns], in0=th[:, ch % 2, ns], scalar=1.0, in1=ffn_banks(ch)[0][:, ns],
                                         op0=ALU.add, op1=ALU.mult).then_inc(s_gated, 1)
                dve.wait_ge(s_up, HC * num(w) + ch + 1)
                dve.wait_ge(s_gated, HC * num(w) + ch + 1)
                if ch < 2:
                    dve.wait_ge(s_y, HC * num(w))
                else:
                    dve.wait_ge(s_y, HC * num(w) + ch - 1)
                dve.scalar_tensor_tensor(out=hT[:, ch % 2, ns], in0=gated[:, ns], scalar=0.5, in1=ffn_banks(ch)[1][:, ns],
                                         op0=ALU.mult, op1=ALU.mult).then_inc(s_h, 1)

            def d_final(w):
                p0, p1 = places(w)
                dve.wait_ge(s_y, HC * (num(w) + 1))
                if isinstance(w[0], int) and num(w) == G:
                    dve.wait_ge(s_resid, 2 * G)
                else:
                    dve.wait_ge(s_resid, 2 * num(w) + 1)
                dve.tensor_tensor(x_s[:, window_cols(w)], ffn_y[:, p0 * D:p1 * D],
                                  resid[:, w[1], p0:p1, :].rearrange("l b d -> l (b d)"), ALU.add).then_inc(s_fin, 1)

            def setup(g):
                if num(g) == 0:
                    dve.wait_ge(s_attnw, 16)
                    dve.tensor_copy(qk_hi[:], attn_w_s[:, 0:2, :]).then_inc(s_whi, 1)
                dve.memset(qs[g[1]][:].bitcast(F32), 0.0).then_inc(s_zeroq[g[1]], 1)

            def step(p, c, b, a, v=None, late=None):
                for s in range(FIRST_SLOT, LAST_SLOT + 1):
                    if a is not None and s == MS_SLOT:
                        a_mean(a, c)
                        if c is None:
                            setup(a)
                    for g, at in in_slot(p, c, s):
                        for n in range(NB):
                            if at == 4 * n + NORM:
                                c_norm(g, n)
                            if at == 4 * n + X1:
                                c_x1(g, n)
                            if at == 4 * n + HI2:
                                d_hi(g, n)
                    for w, first in windows(p, c, late):
                        if 0 <= s - first < HC:
                            d_hidden(w, s - first)
                        if s == first + HC:
                            d_final(w)
                    if b is not None and 0 <= s - RAW_LAG < NK:
                        b_max(b, s - RAW_LAG)
                    if a is not None and s in (HI1, HI1 + 8):
                        a_hi(a, (s - HI1) // 8)
                    if b is not None and s == SHIFT_SLOT:
                        b_shift(b)
                    if a is not None and s == QREST:
                        a_rest(a, score[0], qp, q_rest, s_qhi, s_qlo, s_qrest)
                    if a is not None and s == KREST:
                        a_rest(a, score[1], kp, k_rest, s_khi, s_klo, s_krest)

            def weights():
                dve.wait_ge(s_ffnin, 16)
                dve.tensor_copy(ffn_hi[:], ffn_in_s[:]).then_inc(s_whi, 1)

            dve.memset(va[0][:], 0.0).then_inc(s_va0[0], 1)
            dve.memset(ones[:], 1.0).then_inc(s_ones, 1)
            dve.wait_ge(s_va0[0], 1)
            dve.memset(va[0][:, :, :, DH:DH + 1], 1.0).then_inc(s_va0[0], 1)
            run_steps(dve, step, weights)

        @block.gpsimd
        def _(pool):
            def a_inv(g):
                pool.wait_ge(s_ms1, num(g) + 1)
                pool.wait_ge(s_xs1, num(g))
                pool.tensor_tensor(inv1[:], ms1[:], mhalf[:], ALU.pow).then_inc(s_inv1, 1)

            def a_scale(g):
                pool.wait_ge(s_inv1, num(g) + 1)
                pool.wait_ge(s_xt1, NB * num(g))
                pool.tensor_tensor(xs1[:], x_s[:, cols(g)].rearrange("l (b d) -> l b d", b=NB),
                                   inv1[:].unsqueeze(2).to_broadcast([L, NB, D]), ALU.mult).then_inc(s_xs1, 1)

            def a_lo(g, n):
                pool.wait_ge(s_hi1, 2 * num(g) + n + 1)
                if n == 0:
                    pool.wait_ge(s_k, num(g))
                at = slice(2 * n * L, 2 * (n + 1) * L)
                pool.tensor_tensor(xn1_lo[:, at], xn1[:, 2 * n:2 * n + 2, :].rearrange("d b l -> d (b l)"),
                                   xn1_hi[:, at].bitcast(F32), ALU.subtract).then_inc(s_lo1, 1)

            def a_lowest(g, rest, parts, mid, done):
                pool.wait_ge(mid, num(g) + 1)
                before = plus(g, -1)
                if not (isinstance(g[0], int) and num(g) == 0):
                    pool.wait_ge(s_stack[before[1]], STK * (before[0] + 1))
                pool.tensor_tensor(parts[:, 2, :], rest[:], parts[:, 1, :], ALU.subtract).then_inc(done, 1)

            def d_inv(g, b):
                pool.wait_ge(s_ms2, NB * num(g) + b + 1)
                pool.wait_ge(s_xs2, NB * num(g))
                pool.tensor_tensor(inv2[:, b:b + 1], ms2[:, b:b + 1], mhalf[:, 0:1], ALU.pow).then_inc(s_inv2, 1)

            def d_scale(g, b):
                pool.wait_ge(s_inv2, NB * num(g) + b + 1)
                pool.wait_ge(s_xt2, NB * num(g))
                pool.tensor_tensor(xs2[:, b, :], x1[:, b, :], inv2[:, b:b + 1].to_broadcast([L, D]),
                                   ALU.mult).then_inc(s_xs2, 1)

            def d_lo(g, b):
                pool.wait_ge(s_hi2, NB * num(g) + b + 1)
                if b == HALF:
                    pool.wait_ge(s_up, HC * num(g))
                u, p = in_window(g, b)
                pool.tensor_tensor(xn2_lo[:, u, p, :], xn2[:, b, :], xn2_hi[:, u, p, :].bitcast(F32),
                                   ALU.subtract).then_inc(s_lo2, 1)

            def d_resid(g, b):
                pool.wait_ge(s_x1, NB * num(g) + b + HALF)
                if b == HALF:
                    pool.wait_ge(s_fin, num(g))
                u, p = in_window(g, b)
                pool.tensor_tensor(resid[:, u, p:p + HALF, :], x1[:, b:b + HALF, :],
                                   x_s[:, bass.ds(num(g) * W + b * D, HALF * D)].rearrange("l (b d) -> l b d", b=HALF),
                                   ALU.add).then_inc(s_resid, 1)

            def step(p, c, b, a, v=None, late=None):
                for s in range(FIRST_SLOT, LAST_SLOT + 1):
                    for g, at in in_slot(p, c, s):
                        for n in range(NB):
                            if at == 4 * n + X1:
                                d_inv(g, n)
                                d_scale(g, n)
                            if at == 4 * n + HI2:
                                d_lo(g, n)
                            if at == 4 * n + X1 + 2 and n % HALF == HALF - 1:
                                d_resid(g, n + 1 - HALF)
                    if a is not None and s == MS_SLOT:
                        a_inv(a)
                        a_scale(a)
                        if first(a):
                            pool.wait_ge(s_whi, 1)
                            pool.tensor_tensor(qk_lo[:], attn_w_s[:, 0:2, :], qk_hi[:].bitcast(F32),
                                               ALU.subtract).then_inc(s_wlo, 1)
                    if a is not None and s in (HI1, HI1 + 8):
                        a_lo(a, (s - HI1) // 8)
                        if first(a) and s > HI1:
                            pool.memset(ks[1][:].bitcast(F32), 0.0).then_inc(s_zerok[1], 1)
                    if a is not None and s == QLO:
                        a_lowest(a, q_rest, qp, s_qmid, s_qlo)
                    if a is not None and s == KLO:
                        a_lowest(a, k_rest, kp, s_kmid, s_klo)

            def rest():
                pool.memset(va[1][:], 0.0).then_inc(s_va0[1], 1)
                pool.wait_ge(s_va0[1], 1)
                pool.memset(va[1][:, :, :, DH:DH + 1], 1.0).then_inc(s_va0[1], 1)
                pool.wait_ge(s_whi, 2)
                pool.tensor_tensor(ffn_lo[:], ffn_in_s[:], ffn_hi[:].bitcast(F32), ALU.subtract).then_inc(s_wlo, 1)

            pool.memset(mhalf[:], -0.5).then_inc(s_mhalf, 1)
            pool.memset(ident[:], 0.0).then_inc(s_ident0, 1)
            pool.memset(nmax[:], 0.0).then_inc(s_nmax0, 1)
            pool.wait_ge(s_ident0, 1)
            pool.affine_select(out=ident[:], in_=ident[:], compare_op=ALU.not_equal, fill=1.0, base=0,
                               pattern=[[-1, 128]], channel_multiplier=1).then_inc(s_ident, 1)
            pool.memset(ks[0][:].bitcast(F32), 0.0).then_inc(s_zerok[0], 1)
            pool.wait_ge(s_mhalf, 1)
            run_steps(pool, step, rest)


def kernel(x, cond_256, L0_cond_Wq, L0_cond_Wk, L0_cond_Wv, L0_cond_Wo, L0_cond_g1w, L0_cond_g1b, L0_cond_b1w,
           L0_cond_b1b, L0_cond_g2w, L0_cond_g2b, L0_cond_b2w, L0_cond_b2b, L0_cond_gate_w, L0_cond_hid_w,
           L0_cond_out_w):
    import numpy as np
    import concourse.bacc as bacc
    from concourse.bass_utils import run_bass_kernel_spmd

    heads, dim = 16, 128
    x, cond = np.asarray(x), np.asarray(cond_256)
    wq, wk, wv, wo = (np.asarray(w) for w in (L0_cond_Wq, L0_cond_Wk, L0_cond_Wv, L0_cond_Wo))

    def dim_head(w):
        return w.reshape(heads, dim // heads, dim).transpose(1, 0, 2).reshape(dim, dim)

    hid = np.asarray(L0_cond_gate_w).shape[0]
    arrays = {
        "x": x.transpose(1, 0, 2),
        "cond": cond.T,
        "mod_w": np.stack([np.asarray(w).T for w in (L0_cond_g1w, L0_cond_b1w, L0_cond_g2w, L0_cond_b2w)], axis=1),
        "mod_b": np.stack([np.asarray(b) for b in (L0_cond_g1b, L0_cond_b1b, L0_cond_g2b, L0_cond_b2b)], axis=1),
        "attn_w": np.stack([dim_head(wq).T, dim_head(wk).T, wv.T, wo.T], axis=1),
        "ffn_in_w": np.stack([np.asarray(L0_cond_gate_w).T, np.asarray(L0_cond_hid_w).T], axis=1),
        "ffn_out_w": np.asarray(L0_cond_out_w).T.reshape(hid // 128, 128, dim).transpose(1, 0, 2),
    }
    arrays = {f"in_{n}": np.ascontiguousarray(a) for n, a in arrays.items()}
    nc = bacc.Bacc("TRN2", target_bir_lowering=False, num_devices=1)
    aps = [nc.dram_tensor(n, a.shape, mybir.dt.from_np(a.dtype), kind="ExternalInput").ap() for n, a in arrays.items()]
    batch, length, _ = x.shape
    out = nc.dram_tensor("out_y", (length, batch, dim), F32, kind="ExternalOutput").ap()
    bass_cond_transformer_block(nc, *aps, out)
    r = run_bass_kernel_spmd(nc, [arrays], core_ids=[0])
    return np.ascontiguousarray(r.results[0]["out_y"].transpose(1, 0, 2))
```

```python
from contextlib import ExitStack

import concourse.bass as bass
from concourse import mybir

ALU = mybir.AluOpType
ACT = mybir.ActivationFunctionType
AX = mybir.AxisListType
F32 = mybir.dt.float32
F32R = mybir.dt.float32r
BF16 = mybir.dt.bfloat16

EPS = 1e-6


def bass_cond_transformer_block(
    nc: bass.Bass,
    x: bass.AP,
    cond: bass.AP,
    mod_w: bass.AP,
    mod_b: bass.AP,
    attn_w: bass.AP,
    ffn_in_w: bass.AP,
    ffn_out_w: bass.AP,
    out: bass.AP,
):
    L, B, D = x.shape
    DT = cond.shape[0]
    H = 16
    DH = D // H
    HC = ffn_out_w.shape[1]
    NB = 4
    G = B // NB
    W = NB * L
    HQ = 4
    CH = H // HQ
    NK = NB * CH
    NP = 4
    VW = 32
    PARTS = 3
    Q_PART = [0, 0, 0, 1, 1, 2]
    K_PART = [0, 1, 2, 0, 1, 0]
    RAW_ROWS = 96
    SHIFT = RAW_ROWS
    STK = 16 * 2 * len(Q_PART)
    SCALE = float(DH) ** -0.5
    assert D == 128 and L == 128 and W == 512 and B % (2 * NB) == 0 and H * DH == D and HC == 4

    PV_LAG = 2
    RAW_LAG = 3
    OT, TR4, NORM, TRO, OTC, WO, X1 = 6, 7, 8, 9, 10, 10, 11
    XT2, XN2, HI2 = 14, 14, 15
    MS_SLOT = -1
    XT1 = [3, 5, 8, 12]
    HI1 = 5
    Q_SLOT, QHI, QREST = 15, 16, 19
    K_SLOT, KHI, KREST = 18, 19, 20
    V_SLOT = -2
    CT_SLOT = 19
    FFN_SLOT = -2
    FFN_LATE = 5
    FIRST_SLOT, LAST_SLOT = -2, 20
    SLOTS = LAST_SLOT - FIRST_SLOT + 1
    HALF = NB // 2

    ctx = ExitStack()
    with ctx:
        def sb(name, shape, dt=F32):
            return ctx.enter_context(nc.sbuf_tensor(name, shape, dt))

        def bank(name):
            return ctx.enter_context(nc.psum_tensor(name, [128, 512], F32))

        def sem(name):
            return ctx.enter_context(nc.semaphore(name))

        cond_s = sb("cond_s", [DT, B])
        mod_w_s = sb("mod_w_s", [DT, 4, D])
        mod_b_s = sb("mod_b_s", [D, 4])
        attn_w_s = sb("attn_w_s", [D, 4, D])
        ffn_in_s = sb("ffn_in_s", [D, 2, HC * 128])
        ffn_out_s = sb("ffn_out_s", [128, HC, D])
        qk_hi = sb("qk_hi", [D, 2, D], F32R)
        qk_lo = sb("qk_lo", [D, 2, D], F32R)
        ffn_hi = sb("ffn_hi", [D, 2, HC * 128], F32R)
        ffn_lo = sb("ffn_lo", [D, 2, HC * 128], F32R)
        mod = sb("mod", [D, 4, B])
        ident = sb("ident", [128, 128])
        mhalf = sb("mhalf", [128, NB])
        ones = sb("ones", [H * NB, L], BF16)
        x_s = sb("x_s", [L, B * D])
        sqx = sb("sqx", [L, NB, D])
        sq1 = sb("sq1", [L, NB])
        ms1 = sb("ms1", [L, NB])
        inv1 = sb("inv1", [L, NB])
        xs1 = sb("xs1", [L, NB, D])
        xn1 = sb("xn1", [D, NB, L])
        xn1_hi = sb("xn1_hi", [D, W], F32R)
        xn1_lo = sb("xn1_lo", [D, W], F32R)
        qp = sb("qp", [D, PARTS, W], BF16)
        kp = sb("kp", [D, PARTS, W], BF16)
        q_rest = sb("q_rest", [D, W])
        k_rest = sb("k_rest", [D, W])
        qs = [sb(f"qs{u}", [128, H, W], BF16) for u in range(2)]
        ks = [sb(f"ks{u}", [128, H, W], BF16) for u in range(2)]
        va = [sb(f"va{u}", [L, NB, H, VW]) for u in range(2)]
        nmax = sb("nmax", [L, 128])
        shift = sb("shift", [H * NB, 2, L], BF16)
        p_s = sb("p_s", [L, NP, HQ * L])
        ot_s = sb("ot_s", [128, 2, CH * L])
        rden = sb("rden", [L, H])
        o_s = sb("o_s", [L, D])
        oT_s = sb("oT_s", [D, L])
        x1 = sb("x1", [L, NB, D])
        sqx1 = sb("sqx1", [L, NB, D])
        ms2 = sb("ms2", [L, NB])
        inv2 = sb("inv2", [L, NB])
        xs2 = sb("xs2", [L, NB, D])
        xn2 = sb("xn2", [D, NB, L])
        xn2_hi = sb("xn2_hi", [D, 2, NB, L], F32R)
        xn2_lo = sb("xn2_lo", [D, 2, NB, L], F32R)
        th = sb("th", [128, 2, W])
        gated = sb("gated", [128, W])
        hT = sb("hT", [128, 2, W])
        resid = sb("resid", [L, 2, NB, D])

        score = [bank("score0"), bank("score1")]
        gate_up = [bank("gate"), bank("up")]
        pv = [bank("pv0"), bank("pv1")]
        ffn_y = pv[1]
        tok = bank("tok")
        small = bank("small")

        def ffn_banks(ch):
            return score if ch == 1 else gate_up

        s_x = [sem("s_xin0"), sem("s_xin1")]
        s_xrest = sem("s_xrest")
        s_modw, s_modb, s_attnw = sem("s_modw"), sem("s_modb"), sem("s_attnw")
        s_ffnin, s_ffnout = sem("s_ffnin"), sem("s_ffnout")
        s_stack = [sem("s_stack0"), sem("s_stack1")]
        s_shiftrow = [sem("s_shiftrow0"), sem("s_shiftrow1")]
        s_out = sem("s_out")
        s_ident0, s_ident, s_mhalf, s_nmax0, s_ones, s_table = (sem("s_ident0"), sem("s_ident"), sem("s_mhalf"),
                                                                sem("s_nmax0"), sem("s_ones"), sem("s_table"))
        s_va0 = [sem("s_va00"), sem("s_va01")]
        s_onerows = sem("s_onerows")
        s_zeroq, s_zerok = [sem("s_zeroq0"), sem("s_zeroq1")], [sem("s_zerok0"), sem("s_zerok1")]
        s_modp, s_mod, s_whi, s_wlo = sem("s_modp"), sem("s_mod"), sem("s_whi"), sem("s_wlo")
        s_sq1 = sem("s_sq1")
        s_ms1, s_inv1, s_xs1, s_xt1, s_xn1, s_hi1, s_lo1 = (sem("s_ms1"), sem("s_inv1"), sem("s_xs1"), sem("s_xt1"),
                                                            sem("s_xn1"), sem("s_hi1"), sem("s_lo1"))
        s_v, s_va = sem("s_v"), sem("s_va")
        s_q, s_qhi, s_qrest, s_qmid, s_qlo = sem("s_q"), sem("s_qhi"), sem("s_qrest"), sem("s_qmid"), sem("s_qlo")
        s_k, s_khi, s_krest, s_kmid, s_klo = sem("s_k"), sem("s_khi"), sem("s_krest"), sem("s_kmid"), sem("s_klo")
        s_raw, s_max, s_maxT, s_shi, s_slo = sem("s_raw"), sem("s_max"), sem("s_maxT"), sem("s_shi"), sem("s_slo")
        s_score, s_exp, s_pv, s_ot, s_tr4, s_rden = (sem("s_score"), sem("s_exp"), sem("s_pv"), sem("s_ot"),
                                                     sem("s_tr4"), sem("s_rden"))
        s_o, s_oTp, s_oT, s_wo, s_x1 = sem("s_o"), sem("s_oTp"), sem("s_oT"), sem("s_wo"), sem("s_x1")
        s_ms2, s_inv2, s_xs2, s_xt2, s_xn2, s_hi2, s_lo2 = (sem("s_ms2"), sem("s_inv2"), sem("s_xs2"), sem("s_xt2"),
                                                            sem("s_xn2"), sem("s_hi2"), sem("s_lo2"))
        s_gate, s_up, s_tanh, s_gated, s_h, s_y, s_resid, s_fin = (
            sem("s_gate"), sem("s_up"), sem("s_tanh"), sem("s_gated"), sem("s_h"), sem("s_y"), sem("s_resid"),
            sem("s_fin"))

        def num(g):
            return g[0] * 2 + g[1]

        def plus(g, n):
            return (g[0] + (g[1] + n) // 2, (g[1] + n) % 2)

        def xt1_bank(c, b):
            return tok if c is None and b % 2 else small

        def is_first(g):
            return isinstance(g[0], int) and num(g) == 0

        def upto(w, n):
            return min(num(w) + n, G) if isinstance(w[0], int) else num(w) + n

        def cols(g):
            return bass.ds(num(g) * W, W)

        def places(w):
            if isinstance(w[0], int):
                return {0: (HALF, NB), G: (0, HALF)}.get(num(w), (0, NB))
            return 0, NB

        def window_cols(w):
            p0, p1 = places(w)
            return bass.ds(num(w) * W + (p0 - HALF) * D, (p1 - p0) * D)

        def in_window(g, b):
            return (g[1] + (b >= HALF)) % 2, (b + HALF) % NB

        def run_steps(eng, step):
            last = (G // 2 - 1, 1)
            step(None, None, None, (0, 0))
            step(None, None, None, (0, 1), v=(0, 0))
            step(None, None, (0, 0), None, v=(0, 1))
            step(None, (0, 0), (0, 1), (1, 0))
            step((0, 0), (0, 1), (1, 0), (1, 1), v=(1, 0))
            with eng.Fori(1, G // 2 - 1) as i:
                for u in range(2):
                    step(plus((i, u), -1), (i, u), plus((i, u), 1), plus((i, u), 2), v=plus((i, u), 1))
            step(plus(last, -2), plus(last, -1), last, None, v=last)
            step(plus(last, -1), last, None, None)
            step(last, None, None, None, late=(G // 2, 0))

        def in_slot(p, c, s):
            return ([] if p is None else [(p, s + SLOTS)]) + ([] if c is None else [(c, s)])

        def windows(p, c, late):
            return ([(p, FFN_SLOT)] if p is not None else []) + (
                [(late, FFN_LATE)] if late is not None else [])

        block = ctx.enter_context(nc.Block())

        @block.sync
        def _(sp):
            def ahead(value):
                return value if isinstance(value, int) else sp.compute_val(value)

            def stack_rows(g, n, dst, parts, part_of, part, ready):
                sp.wait_ge(ready, n)
                for r in range(len(part_of)):
                    if part_of[r] == part:
                        sp.dma_start(dst[g[1]][DH * r:DH * r + DH, :, :].rearrange("d h w -> d (h w)"),
                                     parts[:, part, :]).then_inc(s_stack[g[1]], 16)

            def step(p, c, b, a, v=None, late=None):
                stores = []
                for w, _ in windows(p, c, late):
                    p0, p1 = places(w)
                    stores.append((ahead(num(w) * W + (p0 - HALF) * D), (p1 - p0) * D, ahead(num(w) + 1)))
                if c is not None:
                    scores_before, scores_done = ahead(NK * num(c)), ahead(NK * (num(c) + 1))
                if b is not None:
                    b_done = ahead(num(b) + 1)
                if a is not None:
                    a_done = ahead(num(a) + 1)
                for at, width, done in stores:
                    sp.wait_ge(s_fin, done)
                    sp.dma_start(out.rearrange("l b d -> l (b d)")[:, bass.ds(at, width)],
                                 x_s[:, bass.ds(at, width)]).then_inc(s_out, 16)
                if b is not None:
                    if c is not None:
                        sp.wait_ge(s_score, scores_before)
                    sp.wait_ge(s_shi, b_done)
                    sp.dma_start(qs[b[1]][SHIFT:SHIFT + 1, :, :].rearrange("d h w -> d (h w)"),
                                 shift[:, 0, :]).then_inc(s_shiftrow[b[1]], 16)
                    sp.wait_ge(s_slo, b_done)
                    sp.dma_start(qs[b[1]][SHIFT + 1:SHIFT + 2, :, :].rearrange("d h w -> d (h w)"),
                                 shift[:, 1, :]).then_inc(s_shiftrow[b[1]], 16)
                if a is not None:
                    if c is not None:
                        sp.wait_ge(s_score, scores_done)
                    else:
                        sp.wait_ge(s_zeroq[a[1]], 2)
                        sp.wait_ge(s_zerok[a[1]], 1)
                        sp.wait_ge(s_ones, 1)
                        for row in (SHIFT, SHIFT + 1):
                            sp.dma_start(ks[a[1]][row:row + 1, :, :].rearrange("d h w -> d (h w)"),
                                         ones[:]).then_inc(s_onerows, 16)
                    stack_rows(a, a_done, qs, qp, Q_PART, 0, s_qhi)
                    stack_rows(a, a_done, qs, qp, Q_PART, 1, s_qmid)
                    stack_rows(a, a_done, ks, kp, K_PART, 0, s_khi)
                    stack_rows(a, a_done, ks, kp, K_PART, 1, s_kmid)
                    stack_rows(a, a_done, qs, qp, Q_PART, 2, s_qlo)
                    stack_rows(a, a_done, ks, kp, K_PART, 2, s_klo)

            x_cols = x.rearrange("l b d -> l (b d)")
            sp.dma_start(x_s[:, 0:W], x_cols[:, 0:W]).then_inc(s_x[0], 16)
            sp.dma_start(mod_b_s[:], mod_b).then_inc(s_modb, 16)
            sp.dma_start(attn_w_s[:], attn_w).then_inc(s_attnw, 16)
            sp.dma_start(x_s[:, W:2 * W], x_cols[:, W:2 * W]).then_inc(s_x[1], 16)
            sp.dma_start(ffn_in_s[:], ffn_in_w).then_inc(s_ffnin, 16)
            sp.dma_start(ffn_out_s[:], ffn_out_w).then_inc(s_ffnout, 16)
            sp.dma_start(x_s[:, 2 * W:], x_cols[:, 2 * W:]).then_inc(s_xrest, 16)

            run_steps(sp, step)
            sp.wait_ge(s_out, 16 * (G + 1))

        @block.tensor
        def _(pe):
            def split_product(dst, w_hi, w_lo, v_hi, v_lo):
                pe.matmul(dst, w_hi, v_hi, start=True, stop=False)
                pe.matmul(dst, w_hi, v_lo, start=False, stop=False)
                return pe.matmul(dst, w_lo, v_hi, start=False, stop=True)

            def a_transpose(g, c, b):
                pe.wait_ge(s_xs1, num(g) + 1)
                pe.wait_ge(s_xn1, NB * num(g) + (b if c is not None else max(b - 1, 0)))
                if c is not None and b == 0:
                    pe.wait_ge(s_x1, NB * num(c))
                if c is not None and b == 3:
                    pe.wait_ge(s_x1, NB * num(c) + 1)
                pe.transpose(xt1_bank(c, b)[:, 0:L], xs1[:, b, :], ident[:]).then_inc(s_xt1, 1)

            def a_values(g, c):
                pe.wait_ge(s_xn1, NB * (num(g) + 1))
                pe.wait_ge(s_va, num(g))
                if c is not None:
                    pe.wait_ge(s_slo, num(g))
                for b in range(NB):
                    mm = pe.matmul(pv[0][:, b * L:(b + 1) * L], xn1[:, b, :], attn_w_s[:, 2, :], start=True, stop=True)
                mm.then_inc(s_v, 1)

            def a_query(g, c):
                if c is not None:
                    pe.wait_ge(s_exp, NK * (num(c) + 1) - 1)
                else:
                    pe.wait_ge(s_qrest, num(g))
                pe.wait_ge(s_lo1, 2 * (num(g) + 1))
                if is_first(g):
                    pe.wait_ge(s_wlo, 1)
                split_product(score[0][:], qk_hi[:, 0, :], qk_lo[:, 0, :], xn1_hi[:], xn1_lo[:]).then_inc(s_q, 1)

            def a_key(g, c):
                if c is not None:
                    pe.wait_ge(s_exp, NK * (num(c) + 1))
                else:
                    pe.wait_ge(s_krest, num(g))
                split_product(score[1][:], qk_hi[:, 1, :], qk_lo[:, 1, :], xn1_hi[:], xn1_lo[:]).then_inc(s_k, 1)

            def b_raw(g, p, k):
                b, ch = k // CH, k % CH
                if k == 0:
                    pe.wait_ge(s_stack[g[1]], STK * (g[0] + 1))
                    if p is not None:
                        pe.wait_ge(s_h, HC * (num(p) + 1))
                if k >= 2:
                    pe.wait_ge(s_max, NK * num(g) + k - 1)
                for j in range(HQ):
                    h = ch * HQ + j
                    mm = pe.matmul(gate_up[k % 2][:, j * L:(j + 1) * L], qs[g[1]][0:RAW_ROWS, h, b * L:(b + 1) * L],
                                   ks[g[1]][0:RAW_ROWS, h, b * L:(b + 1) * L], start=True, stop=True)
                mm.then_inc(s_raw, 1)

            def b_maxT(g, c):
                pe.wait_ge(s_max, NK * (num(g) + 1))
                if c is None:
                    pe.wait_ge(s_nmax0, 1)
                    pe.wait_ge(s_va, 2)
                else:
                    pe.wait_ge(s_ot, NB * num(c) + 3)
                pe.transpose(pv[0][:, 0:L], nmax[:], ident[:]).then_inc(s_maxT, 1)

            def c_scores(g, p, k):
                b, ch = k // CH, k % CH
                if k == 0:
                    pe.wait_ge(s_shiftrow[g[1]], 32 * (g[0] + 1))
                    pe.wait_ge(s_exp, NK * num(g))
                    ready = upto(g, 2)
                    pe.wait_ge(s_qrest, ready)
                    pe.wait_ge(s_krest, ready)
                    if is_first(g):
                        pe.wait_ge(s_onerows, 64)
                    if p is not None:
                        pe.wait_ge(s_h, HC * num(p) + 2)
                if k >= 2:
                    pe.wait_ge(s_exp, NK * num(g) + k - 1)
                for j in range(HQ):
                    h = ch * HQ + j
                    mm = pe.matmul(score[k % 2][:, j * L:(j + 1) * L], ks[g[1]][:, h, b * L:(b + 1) * L],
                                   qs[g[1]][:, h, b * L:(b + 1) * L], start=True, stop=True)
                mm.then_inc(s_score, 1)

            def c_pv(g, p, k):
                b, ch = k // CH, k % CH
                if k == 0:
                    pe.wait_ge(s_va, upto(g, 2))
                    pe.wait_ge(s_slo, num(g) + 1)
                    pe.wait_ge(s_ot, NB * num(g))
                if k == CH and p is not None:
                    pe.wait_ge(s_fin, num(p) + 1)
                if ch == 0 and b >= 2:
                    pe.wait_ge(s_ot, NB * num(g) + b - 1)
                pe.wait_ge(s_exp, NK * num(g) + k + 1)
                for j in range(HQ):
                    h = ch * HQ + j
                    mm = pe.matmul(pv[b % 2][VW * j:VW * j + VW, ch * L:(ch + 1) * L], va[g[1]][:, b, h, :],
                                   p_s[:, k % NP, j * L:(j + 1) * L], start=True, stop=True)
                mm.then_inc(s_pv, 1)

            def c_tr4(g, b):
                pe.wait_ge(s_ot, NB * num(g) + b + 1)
                pe.wait_ge(s_o, NB * num(g) + b)
                pe.wait_ge(s_xn2, NB * num(g) + max(b - 1, 0))
                for ch in range(CH):
                    mm = pe.transpose(tok[:, ch * 128:(ch + 1) * 128], ot_s[:, b % 2, ch * L:(ch + 1) * L], ident[:])
                mm.then_inc(s_tr4, 1)

            def c_tro(g, b, a):
                pe.wait_ge(s_o, NB * num(g) + b + 1)
                pe.wait_ge(s_x1, NB * num(g) + b)
                if a is not None and b < 2:
                    pe.wait_ge(s_xn1, NB * num(a) + b + 3)
                pe.transpose(small[:, 0:L], o_s[:], ident[:]).then_inc(s_oTp, 1)

            def c_wo(g, b):
                pe.wait_ge(s_oT, NB * num(g) + b + 1)
                pe.matmul(small[:, L:2 * L], oT_s[:], attn_w_s[:, 3, :], start=True, stop=True).then_inc(s_wo, 1)

            def d_xt2(g, b):
                pe.wait_ge(s_xs2, NB * num(g) + b + 1)
                pe.wait_ge(s_o, NB * num(g) + min(b + 2, NB))
                pe.wait_ge(s_xn2, NB * num(g) + b)
                pe.transpose(tok[:, 0:L], xs2[:, b, :], ident[:]).then_inc(s_xt2, 1)

            def d_gate_up(w, ch):
                if is_first(w) and ch == 0:
                    pe.wait_ge(s_wlo, 2)
                if ch == 0:
                    pe.wait_ge(s_lo2, NB * upto(w, 0) + (HALF if places(w)[1] == NB else 0))
                    pe.wait_ge(s_max, NK * upto(w, 2))
                    pe.wait_ge(s_h, HC * num(w))
                elif ch == 1:
                    pe.wait_ge(s_qrest, upto(w, 3))
                    pe.wait_ge(s_krest, upto(w, 3))
                    pe.wait_ge(s_exp, NK * upto(w, 1))
                    pe.wait_ge(s_h, HC * num(w))
                else:
                    before = {2: 0, 3: 2}[ch]
                    pe.wait_ge(s_gated, HC * num(w) + before + 1)
                p0, p1 = places(w)
                cs, ns = slice(ch * 128, ch * 128 + 128), slice(p0 * L, p1 * L)
                hi, lo = (x[:, w[1], p0:p1, :].rearrange("d b l -> d (b l)") for x in (xn2_hi, xn2_lo))
                gate, up = ffn_banks(ch)
                split_product(gate[:, ns], ffn_hi[:, 0, cs], ffn_lo[:, 0, cs], hi, lo).then_inc(s_gate, 1)
                if ch > 1:
                    pe.wait_ge(s_h, HC * num(w) + before + 1)
                split_product(up[:, ns], ffn_hi[:, 1, cs], ffn_lo[:, 1, cs], hi, lo).then_inc(s_up, 1)

            def d_out(w, ch):
                if is_first(w) and ch == 0:
                    pe.wait_ge(s_ffnout, 16)
                if ch == 0:
                    pe.wait_ge(s_ot, NB * upto(w, 1))
                    pe.wait_ge(s_fin, num(w))
                pe.wait_ge(s_h, HC * num(w) + ch + 1)
                p0, p1 = places(w)
                for p in range(p0, p1):
                    mm = pe.matmul(ffn_y[:, p * D:(p + 1) * D], hT[:, ch % 2, p * L:(p + 1) * L], ffn_out_s[:, ch, :],
                                   start=(ch == 0 and p == p0), stop=(ch == HC - 1), skip_group_check=True)
                mm.then_inc(s_y, 1)

            def step(p, c, b, a, v=None, late=None):
                for s in range(FIRST_SLOT, LAST_SLOT + 1):
                    for w, first in windows(p, c, late):
                        if 0 <= s - first < HC:
                            d_gate_up(w, s - first)
                    if a is not None and s in XT1:
                        a_transpose(a, c, XT1.index(s))
                    if c is not None and 0 <= s < NK:
                        c_scores(c, p, s)
                    if c is not None and 0 <= s - PV_LAG < NK:
                        c_pv(c, p, s - PV_LAG)
                    for w, first in windows(p, c, late):
                        if 0 <= s - first - 1 < HC:
                            d_out(w, s - first - 1)
                    if b is not None and 0 <= s - RAW_LAG < NK:
                        b_raw(b, p, s - RAW_LAG)
                    if v is not None and s == V_SLOT:
                        a_values(v, c)
                    for g, at in in_slot(p, c, s):
                        for n in range(NB):
                            if at == 4 * n + TR4:
                                c_tr4(g, n)
                            if at == 4 * n + TRO:
                                c_tro(g, n, a)
                            if at == 4 * n + WO:
                                c_wo(g, n)
                            if at == 4 * n + XT2:
                                d_xt2(g, n)
                    if b is not None and s == CT_SLOT:
                        b_maxT(b, c)
                    if a is not None and s == Q_SLOT:
                        a_query(a, c)
                    if a is not None and s == K_SLOT:
                        a_key(a, c)

            pe.wait_ge(s_modw, 32)
            for i in range(4):
                mm = pe.matmul(small[:, i * B:(i + 1) * B], mod_w_s[:, i, :], cond_s[:], start=True, stop=True)
            mm.then_inc(s_modp, 1)
            pe.wait_ge(s_mod, 4)
            pe.wait_ge(s_ident, 1)
            run_steps(pe, step)

        @block.scalar
        def _(act):
            def a_norm(g, c, b):
                act.wait_ge(s_xt1, NB * num(g) + b + 1)
                if b == 0:
                    act.wait_ge(s_v, num(g))
                    act.wait_ge(s_lo1, 2 * num(g))
                act.activation(xn1[:, b, :], xt1_bank(c, b)[:, 0:L], ACT.Identity,
                               scale=mod[:, 0, bass.ds(num(g) * NB + b, 1)],
                               bias=mod[:, 1, bass.ds(num(g) * NB + b, 1)]).then_inc(s_xn1, 1)

            def a_values(g):
                act.wait_ge(s_v, num(g) + 1)
                if isinstance(g[0], int) and num(g) < 2:
                    act.wait_ge(s_va0[num(g)], 2)
                else:
                    act.wait_ge(s_pv, NK * (num(g) - 1))
                act.activation(va[g[1]][:, :, :, 0:DH].rearrange("l b h d -> l (b h) d"),
                               pv[0][:].rearrange("l (n d) -> l n d", d=DH), ACT.Copy).then_inc(s_va, 1)

            def a_high(g, ready, src, dst, done):
                act.wait_ge(ready, num(g) + 1)
                before = plus(g, -1)
                if not (isinstance(g[0], int) and num(g) == 0):
                    act.wait_ge(s_stack[before[1]], STK * (before[0] + 1))
                act.activation(dst[:, 0, :], src[:], ACT.Copy).then_inc(done, 1)

            def a_middle(g, ready, rest, dst, done):
                act.wait_ge(ready, num(g) + 1)
                act.activation(dst[:, 1, :], rest[:], ACT.Copy).then_inc(done, 1)

            def c_exp(g, k):
                act.wait_ge(s_score, NK * num(g) + k + 1)
                if k == 0:
                    act.wait_ge(s_pv, NK * num(g))
                if k >= NP:
                    act.wait_ge(s_pv, NK * num(g) + k - NP + 1)
                act.activation(p_s[:, k % NP, :], score[k % 2][:], ACT.Exp, scale=SCALE).then_inc(s_exp, 1)

            def c_ot(g, b):
                act.wait_ge(s_pv, NK * num(g) + CH * (b + 1))
                if b >= 2:
                    act.wait_ge(s_tr4, NB * num(g) + b - 1)
                else:
                    act.wait_ge(s_tr4, NB * num(g))
                act.activation(ot_s[:, b % 2, :], pv[b % 2][:], ACT.Copy).then_inc(s_ot, 1)

            def c_oT(g, b):
                act.wait_ge(s_oTp, NB * num(g) + b + 1)
                act.wait_ge(s_wo, NB * num(g) + b)
                act.activation(oT_s[:], small[:, 0:L], ACT.Copy).then_inc(s_oT, 1)

            def d_norm(g, b):
                act.wait_ge(s_xt2, NB * num(g) + b + 1)
                act.wait_ge(s_lo2, NB * num(g))
                act.activation(xn2[:, b, :], tok[:, 0:L], ACT.Identity,
                               scale=mod[:, 2, bass.ds(num(g) * NB + b, 1)],
                               bias=mod[:, 3, bass.ds(num(g) * NB + b, 1)]).then_inc(s_xn2, 1)

            def d_tanh(w, ch):
                if is_first(w) and ch == 0:
                    act.wait_ge(s_table, 1)
                act.wait_ge(s_gate, HC * num(w) + ch + 1)
                if ch < 2:
                    act.wait_ge(s_gated, HC * num(w))
                else:
                    act.wait_ge(s_gated, HC * num(w) + ch - 1)
                ns = slice(places(w)[0] * L, places(w)[1] * L)
                act.activation(th[:, ch % 2, ns], ffn_banks(ch)[0][:, ns], ACT.Tanh, scale=0.5).then_inc(s_tanh, 1)

            def zero_stack(u):
                act.activation(qs[u][:, H // 2:, :].bitcast(F32).rearrange("d h w -> d (h w)"),
                               nmax[:, 0:1].to_broadcast([128, H * W // 4]), ACT.Copy).then_inc(s_zeroq[u], 1)

            def step(p, c, b, a, v=None, late=None):
                for s in range(FIRST_SLOT, LAST_SLOT + 1):
                    for w, first in windows(p, c, late):
                        if 0 <= s - first < HC:
                            d_tanh(w, s - first)
                    for g, at in in_slot(p, c, s):
                        for n in range(NB):
                            if at == 4 * n + OTC:
                                c_oT(g, n)
                            if at == 4 * n + OT:
                                c_ot(g, n)
                    if a is not None and s in XT1:
                        a_norm(a, c, XT1.index(s))
                        if is_first(a) and s == XT1[-1]:
                            zero_stack(1)
                    if c is not None and 0 <= s < NK:
                        c_exp(c, s)
                    for g, at in in_slot(p, c, s):
                        for n in range(NB):
                            if at == 4 * n + XN2:
                                d_norm(g, n)
                    if v is not None and s == V_SLOT:
                        a_middle(v, s_qrest, q_rest, qp, s_qmid)
                        a_middle(v, s_krest, k_rest, kp, s_kmid)
                        a_values(v)
                    if a is not None and s == QHI:
                        a_high(a, s_q, score[0], qp, s_qhi)
                    if a is not None and s == KHI:
                        a_high(a, s_k, score[1], kp, s_khi)

            act.dma_start(mod_w_s[:], mod_w).then_inc(s_modw, 16)
            act.dma_start(cond_s[:], cond).then_inc(s_modw, 16)
            act.wait_ge(s_mhalf, 1)
            act.activation(th[:, 0, 0:NB], mhalf[:], ACT.Exp).then_inc(s_table, 1)
            act.wait_ge(s_nmax0, 1)
            zero_stack(0)
            act.wait_ge(s_modp, 1)
            act.wait_ge(s_modb, 16)
            for i in range(4):
                act.activation(mod[:, i, :], small[:, i * B:(i + 1) * B], ACT.Identity,
                               bias=mod_b_s[:, i:i + 1]).then_inc(s_mod, 1)
            act.wait_ge(s_mod, 4)
            run_steps(act, step)

        @block.vector
        def _(dve):
            def a_mean(g, c):
                if c is None:
                    dve.wait_ge(s_x[g[1]], 16)
                else:
                    dve.wait_ge(s_xrest, 16)
                dve.wait_ge(s_ms1, num(g))
                for b in range(NB):
                    xb = x_s[:, bass.ds(num(g) * W + b * D, D)]
                    dve.scalar_tensor_tensor(out=sqx[:, b, :], in0=xb, scalar=1.0 / D, in1=xb,
                                             op0=ALU.mult, op1=ALU.mult, accum_out=sq1[:, b:b + 1]).then_inc(s_sq1, 1)
                dve.wait_ge(s_sq1, NB * (num(g) + 1))
                dve.wait_ge(s_inv1, num(g))
                dve.tensor_scalar(ms1[:], sq1[:], EPS, None, ALU.add).then_inc(s_ms1, 1)

            def a_hi(g, n):
                dve.wait_ge(s_xn1, NB * num(g) + 2 * n + 2)
                if n == 0:
                    dve.wait_ge(s_k, num(g))
                    dve.wait_ge(s_lo1, 2 * num(g))
                dve.tensor_copy(xn1_hi[:, 2 * n * L:2 * (n + 1) * L],
                                xn1[:, 2 * n:2 * n + 2, :].rearrange("d b l -> d (b l)")).then_inc(s_hi1, 1)

            def a_rest(g, src, parts, rest, high, lowest, done):
                dve.wait_ge(high, num(g) + 1)
                dve.wait_ge(lowest, num(g))
                dve.tensor_tensor(rest[:], src[:], parts[:, 0, :], ALU.subtract).then_inc(done, 1)

            def b_max(g, k):
                b, ch = k // CH, k % CH
                dve.wait_ge(s_raw, NK * num(g) + k + 1)
                if k == 0 and is_first(g):
                    dve.wait_ge(s_nmax0, 1)
                    dve.wait_ge(s_zeroq[1], 2)
                if k == 0:
                    dve.wait_ge(s_maxT, num(g))
                heads = nmax[:, ch * HQ * NB:(ch + 1) * HQ * NB].rearrange("l (j b) -> l j b", b=NB)
                dve.tensor_reduce(heads[:, :, b], gate_up[k % 2][:].rearrange("l (j m) -> l j m", j=HQ),
                                  AX.X, ALU.max, negate=True).then_inc(s_max, 1)

            def b_shift(g):
                dve.wait_ge(s_maxT, num(g) + 1)
                before = plus(g, -1)
                if not (isinstance(g[0], int) and num(g) == 0):
                    dve.wait_ge(s_shiftrow[before[1]], 32 * (before[0] + 1))
                dve.tensor_copy(shift[:, 0, :], pv[0][0:H * NB, 0:L]).then_inc(s_shi, 1)
                dve.wait_ge(s_shi, num(g) + 1)
                dve.tensor_tensor(shift[:, 1, :], pv[0][0:H * NB, 0:L], shift[:, 0, :],
                                  ALU.subtract).then_inc(s_slo, 1)

            def c_norm(g, b):
                dve.wait_ge(s_tr4, NB * num(g) + b + 1)
                heads = tok[:].rearrange("l (h v) -> l h v", v=VW)
                dve.reciprocal(rden[:], heads[:, :, DH]).then_inc(s_rden, 1)
                dve.wait_ge(s_rden, NB * num(g) + b + 1)
                dve.wait_ge(s_oTp, NB * num(g) + b)
                dve.tensor_tensor(o_s[:].rearrange("l (h d) -> l h d", h=H), heads[:, :, 0:DH],
                                  rden[:].unsqueeze(2).to_broadcast([L, H, DH]), ALU.mult).then_inc(s_o, 1)

            def c_x1(g, b):
                dve.wait_ge(s_wo, NB * num(g) + b + 1)
                if b == 0:
                    dve.wait_ge(s_resid, 2 * num(g))
                dve.tensor_tensor(x1[:, b, :], small[:, L:2 * L], x_s[:, bass.ds(num(g) * W + b * D, D)],
                                  ALU.add).then_inc(s_x1, 1)
                dve.wait_ge(s_x1, NB * num(g) + b + 1)
                dve.wait_ge(s_ms2, NB * num(g))
                dve.tensor_tensor_reduce(sqx1[:, b, :], x1[:, b, :], x1[:, b, :], 1.0 / D, EPS, ALU.mult, ALU.add,
                                         ms2[:, b:b + 1]).then_inc(s_ms2, 1)

            def d_hi(g, b):
                dve.wait_ge(s_xn2, NB * num(g) + b + 1)
                if b == HALF:
                    dve.wait_ge(s_up, HC * num(g))
                    dve.wait_ge(s_lo2, NB * num(g) + HALF)
                u, p = in_window(g, b)
                dve.tensor_copy(xn2_hi[:, u, p, :], xn2[:, b, :]).then_inc(s_hi2, 1)

            def d_hidden(w, ch):
                ns = slice(places(w)[0] * L, places(w)[1] * L)
                dve.wait_ge(s_tanh, HC * num(w) + ch + 1)
                dve.wait_ge(s_h, HC * num(w) + ch)
                gate, up = ffn_banks(ch)
                dve.scalar_tensor_tensor(out=gated[:, ns], in0=th[:, ch % 2, ns], scalar=1.0, in1=gate[:, ns],
                                         op0=ALU.add, op1=ALU.mult).then_inc(s_gated, 1)
                dve.wait_ge(s_up, HC * num(w) + ch + 1)
                dve.wait_ge(s_gated, HC * num(w) + ch + 1)
                if ch < 2:
                    dve.wait_ge(s_y, HC * num(w))
                else:
                    dve.wait_ge(s_y, HC * num(w) + ch - 1)
                dve.scalar_tensor_tensor(out=hT[:, ch % 2, ns], in0=gated[:, ns], scalar=0.5, in1=up[:, ns],
                                         op0=ALU.mult, op1=ALU.mult).then_inc(s_h, 1)

            def d_final(w):
                p0, p1 = places(w)
                dve.wait_ge(s_y, HC * (num(w) + 1))
                dve.wait_ge(s_resid, 2 * num(w) + (p1 == NB))
                dve.tensor_tensor(x_s[:, window_cols(w)], ffn_y[:, p0 * D:p1 * D],
                                  resid[:, w[1], p0:p1, :].rearrange("l b d -> l (b d)"), ALU.add).then_inc(s_fin, 1)

            def zero_stack(u):
                dve.memset(qs[u][:, 0:H // 2, :].bitcast(F32), 0.0).then_inc(s_zeroq[u], 1)

            def surround_values(u):
                dve.memset(va[u][:], 0.0).then_inc(s_va0[u], 1)
                dve.wait_ge(s_va0[u], 1)
                dve.memset(va[u][:, :, :, DH:DH + 1], 1.0).then_inc(s_va0[u], 1)

            def step(p, c, b, a, v=None, late=None):
                for s in range(FIRST_SLOT, LAST_SLOT + 1):
                    if a is not None and s == MS_SLOT and not (c is None and num(a) == 1):
                        a_mean(a, c)
                    if a is not None and is_first(a):
                        if s == MS_SLOT:
                            dve.wait_ge(s_attnw, 16)
                            dve.tensor_copy(qk_hi[:], attn_w_s[:, 0:2, :]).then_inc(s_whi, 1)
                            zero_stack(0)
                        if s == HI1 + 9:
                            a_mean((0, 1), c)
                            zero_stack(1)
                    if c is not None and is_first(c) and s == 0:
                        dve.wait_ge(s_ffnin, 16)
                        dve.tensor_copy(ffn_hi[:], ffn_in_s[:]).then_inc(s_whi, 1)
                    for g, at in in_slot(p, c, s):
                        for n in range(NB):
                            if at == 4 * n + NORM:
                                c_norm(g, n)
                            if at == 4 * n + X1:
                                c_x1(g, n)
                            if at == 4 * n + HI2:
                                d_hi(g, n)
                    for w, first in windows(p, c, late):
                        if 0 <= s - first < HC:
                            d_hidden(w, s - first)
                        if s == first + HC:
                            d_final(w)
                    if b is not None and 0 <= s - RAW_LAG < NK:
                        b_max(b, s - RAW_LAG)
                    if a is not None and s in (HI1, HI1 + 8):
                        a_hi(a, (s - HI1) // 8)
                        if c is None and num(a) == 1 and s > HI1:
                            surround_values(1)
                    if b is not None and s == CT_SLOT:
                        b_shift(b)
                    if a is not None and s == QREST:
                        a_rest(a, score[0], qp, q_rest, s_qhi, s_qlo, s_qrest)
                    if a is not None and s == KREST:
                        a_rest(a, score[1], kp, k_rest, s_khi, s_klo, s_krest)

            dve.memset(ones[:], 1.0).then_inc(s_ones, 1)
            surround_values(0)
            run_steps(dve, step)

        @block.gpsimd
        def _(pool):
            def a_inv(g):
                pool.wait_ge(s_ms1, num(g) + 1)
                pool.wait_ge(s_xs1, num(g))
                pool.tensor_tensor(inv1[:], ms1[:], mhalf[:], ALU.pow).then_inc(s_inv1, 1)

            def a_scale(g):
                pool.wait_ge(s_inv1, num(g) + 1)
                pool.wait_ge(s_xt1, NB * num(g))
                pool.tensor_tensor(xs1[:], x_s[:, cols(g)].rearrange("l (b d) -> l b d", b=NB),
                                   inv1[:].unsqueeze(2).to_broadcast([L, NB, D]), ALU.mult).then_inc(s_xs1, 1)

            def a_lo(g, n):
                pool.wait_ge(s_hi1, 2 * num(g) + n + 1)
                if n == 0:
                    pool.wait_ge(s_k, num(g))
                at = slice(2 * n * L, 2 * (n + 1) * L)
                pool.tensor_tensor(xn1_lo[:, at], xn1[:, 2 * n:2 * n + 2, :].rearrange("d b l -> d (b l)"),
                                   xn1_hi[:, at].bitcast(F32), ALU.subtract).then_inc(s_lo1, 1)

            def a_lowest(g, rest, parts, mid, done):
                pool.wait_ge(mid, num(g) + 1)
                before = plus(g, -1)
                if not (isinstance(g[0], int) and num(g) == 0):
                    pool.wait_ge(s_stack[before[1]], STK * (before[0] + 1))
                pool.tensor_tensor(parts[:, 2, :], rest[:], parts[:, 1, :], ALU.subtract).then_inc(done, 1)

            def d_inv(g, b):
                pool.wait_ge(s_ms2, NB * num(g) + b + 1)
                pool.wait_ge(s_xs2, NB * num(g))
                pool.tensor_tensor(inv2[:, b:b + 1], ms2[:, b:b + 1], mhalf[:, 0:1], ALU.pow).then_inc(s_inv2, 1)

            def d_scale(g, b):
                pool.wait_ge(s_inv2, NB * num(g) + b + 1)
                pool.wait_ge(s_xt2, NB * num(g))
                pool.tensor_tensor(xs2[:, b, :], x1[:, b, :], inv2[:, b:b + 1].to_broadcast([L, D]),
                                   ALU.mult).then_inc(s_xs2, 1)

            def d_lo(g, b):
                pool.wait_ge(s_hi2, NB * num(g) + b + 1)
                if b == HALF:
                    pool.wait_ge(s_up, HC * num(g))
                u, p = in_window(g, b)
                pool.tensor_tensor(xn2_lo[:, u, p, :], xn2[:, b, :], xn2_hi[:, u, p, :].bitcast(F32),
                                   ALU.subtract).then_inc(s_lo2, 1)

            def d_resid(g, b):
                pool.wait_ge(s_x1, NB * num(g) + b + HALF)
                if b == HALF:
                    pool.wait_ge(s_fin, num(g))
                u, p = in_window(g, b)
                pool.tensor_tensor(resid[:, u, p:p + HALF, :], x1[:, b:b + HALF, :],
                                   x_s[:, bass.ds(num(g) * W + b * D, HALF * D)].rearrange("l (b d) -> l b d", b=HALF),
                                   ALU.add).then_inc(s_resid, 1)

            def step(p, c, b, a, v=None, late=None):
                for s in range(FIRST_SLOT, LAST_SLOT + 1):
                    for g, at in in_slot(p, c, s):
                        for n in range(NB):
                            if at == 4 * n + X1:
                                d_inv(g, n)
                                d_scale(g, n)
                            if at == 4 * n + HI2:
                                d_lo(g, n)
                            if at == 4 * n + X1 + 2 and n % HALF == HALF - 1:
                                d_resid(g, n + 1 - HALF)
                    if a is not None and s == MS_SLOT and not (c is None and num(a) == 1):
                        a_inv(a)
                        a_scale(a)
                        if is_first(a):
                            pool.wait_ge(s_whi, 1)
                            pool.tensor_tensor(qk_lo[:], attn_w_s[:, 0:2, :], qk_hi[:].bitcast(F32),
                                               ALU.subtract).then_inc(s_wlo, 1)
                    if c is not None and is_first(c) and s == 0:
                        pool.wait_ge(s_whi, 2)
                        pool.tensor_tensor(ffn_lo[:], ffn_in_s[:], ffn_hi[:].bitcast(F32),
                                           ALU.subtract).then_inc(s_wlo, 1)
                    if a is not None and s in (HI1, HI1 + 8):
                        a_lo(a, (s - HI1) // 8)
                        if is_first(a) and s > HI1:
                            a_inv((0, 1))
                            a_scale((0, 1))
                            pool.memset(ks[1][:].bitcast(F32), 0.0).then_inc(s_zerok[1], 1)
                    if v is not None and s == V_SLOT:
                        a_lowest(v, q_rest, qp, s_qmid, s_qlo)
                        a_lowest(v, k_rest, kp, s_kmid, s_klo)

            pool.memset(mhalf[:], -0.5).then_inc(s_mhalf, 1)
            pool.memset(ident[:], 0.0).then_inc(s_ident0, 1)
            pool.memset(nmax[:], 0.0).then_inc(s_nmax0, 1)
            pool.wait_ge(s_ident0, 1)
            pool.affine_select(out=ident[:], in_=ident[:], compare_op=ALU.not_equal, fill=1.0, base=0,
                               pattern=[[-1, 128]], channel_multiplier=1).then_inc(s_ident, 1)
            pool.memset(ks[0][:].bitcast(F32), 0.0).then_inc(s_zerok[0], 1)
            pool.wait_ge(s_mhalf, 1)
            run_steps(pool, step)


def kernel(x, cond_256, L0_cond_Wq, L0_cond_Wk, L0_cond_Wv, L0_cond_Wo, L0_cond_g1w, L0_cond_g1b, L0_cond_b1w,
           L0_cond_b1b, L0_cond_g2w, L0_cond_g2b, L0_cond_b2w, L0_cond_b2b, L0_cond_gate_w, L0_cond_hid_w,
           L0_cond_out_w):
    import numpy as np
    import concourse.bacc as bacc
    from concourse.bass_utils import run_bass_kernel_spmd

    heads, dim = 16, 128
    x, cond = np.asarray(x), np.asarray(cond_256)
    wq, wk, wv, wo = (np.asarray(w) for w in (L0_cond_Wq, L0_cond_Wk, L0_cond_Wv, L0_cond_Wo))

    def dim_head(w):
        return w.reshape(heads, dim // heads, dim).transpose(1, 0, 2).reshape(dim, dim)

    hid = np.asarray(L0_cond_gate_w).shape[0]
    arrays = {
        "x": x.transpose(1, 0, 2),
        "cond": cond.T,
        "mod_w": np.stack([np.asarray(w).T for w in (L0_cond_g1w, L0_cond_b1w, L0_cond_g2w, L0_cond_b2w)], axis=1),
        "mod_b": np.stack([np.asarray(b) for b in (L0_cond_g1b, L0_cond_b1b, L0_cond_g2b, L0_cond_b2b)], axis=1),
        "attn_w": np.stack([dim_head(wq).T, dim_head(wk).T, wv.T, wo.T], axis=1),
        "ffn_in_w": np.stack([np.asarray(L0_cond_gate_w).T, np.asarray(L0_cond_hid_w).T], axis=1),
        "ffn_out_w": np.asarray(L0_cond_out_w).T.reshape(hid // 128, 128, dim).transpose(1, 0, 2),
    }
    arrays = {f"in_{n}": np.ascontiguousarray(a) for n, a in arrays.items()}
    nc = bacc.Bacc("TRN2", target_bir_lowering=False, num_devices=1)
    aps = [nc.dram_tensor(n, a.shape, mybir.dt.from_np(a.dtype), kind="ExternalInput").ap() for n, a in arrays.items()]
    batch, length, _ = x.shape
    out = nc.dram_tensor("out_y", (length, batch, dim), F32, kind="ExternalOutput").ap()
    bass_cond_transformer_block(nc, *aps, out)
    r = run_bass_kernel_spmd(nc, [arrays], core_ids=[0])
    return np.ascontiguousarray(r.results[0]["out_y"].transpose(1, 0, 2))
```
